# Optimizing a Trainium2 kernel written in Bass

```python
import numpy as np
import jax
import jax.numpy as jnp

def _softmax(x, axis=-1):
    return jax.nn.softmax(x, axis=axis)

def _gelu(x):
    return jax.nn.gelu(x, approximate=True)

def _silu(x):
    return jax.nn.silu(x)

def _sigmoid(x):
    return jax.nn.sigmoid(x)

def _layernorm(x, axis=-1, eps=1e-05):
    m = jnp.mean(x, axis=axis, keepdims=True)
    v = jnp.var(x, axis=axis, keepdims=True)
    return (x - m) / jnp.sqrt(v + eps)

def _scatter_add(tgt, idx, src, axis=0):
    return tgt.at[idx].add(src)

def _segment_sum(src, seg, n):
    return jax.ops.segment_sum(src, seg, n)
kernel_name = 'mk_adaln_ffn_d4_seqx_r8_acf198'

def setup_inputs(seed: int=0):
    np.random.seed(seed)
    _w = jnp.asarray

    def _rec_inputs():
        import jax
        import jax.numpy as jnp
        _rk = jax.random.key(seed)
        x = -0.0005207 + 1.001 * jax.random.normal(jax.random.fold_in(_rk, 1), (8, 128, 512), jnp.float32)
        _lenS = 128 - jax.random.randint(jax.random.fold_in(_rk, 7), (8,), 0, max(1, 128 // 4) + 1, jnp.int32)
        _lenS2 = 128 - jax.random.randint(jax.random.fold_in(_rk, 8), (8,), 0, max(1, 128 // 4) + 1, jnp.int32)
        itok_Bx16_0_63 = jax.random.randint(jax.random.fold_in(_rk, 11), (8, 16), 0, 64, jnp.int32)
        itok_B_207_1644 = jax.random.randint(jax.random.fold_in(_rk, 12), (8,), 207, 1645, jnp.int32)
        condB_coeff = 0.00219231 + 0.0100837 * jax.random.normal(jax.random.fold_in(_rk, 13), (8,), jnp.float32)
        itok_B_3_7 = jax.random.randint(jax.random.fold_in(_rk, 15), (8,), 3, 8, jnp.int32)
        itok_B_2_6 = jax.random.randint(jax.random.fold_in(_rk, 16), (8,), 2, 7, jnp.int32)
        _validS = jnp.arange(128)[None, :] < _lenS[:, None]
        _validS2 = jnp.arange(128)[None, :] < _lenS2[:, None]
        _causal = jnp.tril(jnp.ones((128, 128), dtype=bool))
        mask_Bx4096x4096_ik1 = jnp.where(jnp.ones((8, 512, 512), dtype=bool), 1, 0).astype(jnp.int32)
        return (x, itok_Bx16_0_63, itok_B_207_1644, condB_coeff, itok_B_3_7, itok_B_2_6, mask_Bx4096x4096_ik1)
    x, itok_Bx16_0_63, itok_B_207_1644, condB_coeff, itok_B_3_7, itok_B_2_6, mask_Bx4096x4096_ik1 = _rec_inputs()

    def _L0_cond_setup():
        import jax, jax.numpy as jnp
        import numpy as np
        B, S, HID = (4, 128, 512)
        D, HQ, HK = (128, 32, 8)
        PAGES, PSIZE, NPP = (64, 32, 16)
        THETA = 10000.0
        EPS = 1e-06
        SCALE = 1.0 / float(np.sqrt(D))

        def _rmsnorm(t, w):
            var = jnp.mean(t * t, axis=-1, keepdims=True)
            return t * jax.lax.rsqrt(var + EPS) * w

        def _rope(t, pos):
            inv_freq = 1.0 / THETA ** (jnp.arange(0, D, 2, dtype=jnp.float32) / D)
            freqs = pos[..., None].astype(jnp.float32) * inv_freq
            cos = jnp.cos(freqs)[:, :, None, :]
            sin = jnp.sin(freqs)[:, :, None, :]
            t1, t2 = (t[..., :D // 2], t[..., D // 2:])
            return jnp.concatenate([t1 * cos - t2 * sin, t2 * cos + t1 * sin], axis=-1)
        key = jax.random.key(seed)
        ks = jax.random.split(key, 10)
        x = jax.random.normal(ks[0], (B, S, HID), jnp.float32)
        Wq = jax.random.normal(ks[1], (HQ * D, HID), jnp.float32) * 0.02
        Wk = jax.random.normal(ks[2], (HK * D, HID), jnp.float32) * 0.02
        Wv = jax.random.normal(ks[3], (HK * D, HID), jnp.float32) * 0.02
        Wo = jax.random.normal(ks[4], (HID, HQ * D), jnp.float32) * 0.02
        q_norm_w = jax.random.uniform(ks[5], (D,), jnp.float32)
        k_norm_w = jax.random.uniform(ks[6], (D,), jnp.float32)
        k_cache = jax.random.normal(ks[7], (PAGES, PSIZE, HK, D), jnp.float32)
        v_cache = jax.random.normal(ks[8], (PAGES, PSIZE, HK, D), jnp.float32)
        block_table = jnp.arange(B * NPP, dtype=jnp.int32).reshape(B, NPP)
        cache_seqlens = jax.random.randint(ks[9], (B,), 0, 475).astype(jnp.int32)
        return dict(x=x, Wq=Wq, Wk=Wk, Wv=Wv, Wo=Wo, q_norm_w=q_norm_w, k_norm_w=k_norm_w, k_cache=k_cache, v_cache=v_cache, block_table=block_table, cache_seqlens=cache_seqlens)
    _L0_cond_all = _L0_cond_setup()
    _L0_cond_in = {k: v for k, v in _L0_cond_all.items() if k in ('Wq', 'Wk', 'Wv', 'Wo', 'q_norm_w', 'k_norm_w', 'k_cache', 'v_cache')}
    del _L0_cond_all

    def _L0_ffn_setup():
        import jax, jax.numpy as jnp
        import numpy as np
        B, S, D_IN, D_OUT = (4, 256, 512, 512)
        key = jax.random.key(seed)
        k_x, k_w, k_s, k_b = jax.random.split(key, 4)
        x = jax.random.normal(k_x, (B, S, D_IN), dtype=jnp.float32)
        weight_int8 = jax.random.randint(k_w, (D_OUT, D_IN), 0, 255, dtype=jnp.int32) - 128
        scale = jax.random.uniform(k_s, (D_OUT,), dtype=jnp.float32) * 0.01 + 0.0001
        bias = jax.random.normal(k_b, (D_OUT,), dtype=jnp.float32)
        return {'x': x, 'weight_int8': weight_int8, 'scale': scale, 'bias': bias}
    _L0_ffn_all = _L0_ffn_setup()
    _L0_ffn_in = {k: v for k, v in _L0_ffn_all.items() if k in ('weight_int8', 'scale', 'bias')}
    del _L0_ffn_all

    def _L1_cond_setup():
        import jax, jax.numpy as jnp
        import numpy as np
        B, S, D_IN, D_OUT = (4, 64, 512, 512)
        key = jax.random.key(seed)
        k1, k2, k3, k4, k5 = jax.random.split(key, 5)
        hidden_states = jax.random.normal(k1, (B, S, D_IN), dtype=jnp.float32)
        W = jax.random.normal(k2, (D_OUT, D_IN), dtype=jnp.float32) * 0.02
        b = jax.random.normal(k3, (D_OUT,), dtype=jnp.float32) * 0.02
        coeff = jax.random.normal(k4, (B,), dtype=jnp.float32) * 0.01
        mask = jax.random.randint(k5, (B, D_IN, D_OUT), 0, 2, dtype=jnp.int32)
        return {'hidden_states': hidden_states, 'W': W, 'b': b, 'coeff': coeff, 'mask': mask}
    _L1_cond_all = _L1_cond_setup()
    _L1_cond_in = {k: v for k, v in _L1_cond_all.items() if k in ('W', 'b')}
    del _L1_cond_all

    def _L1_ffn_setup():
        import jax, jax.numpy as jnp
        import numpy as np
        B, T, D_IN, D_OUT = (8, 256, 512, 512)
        N_LORAS, RANK = (16, 32)
        SCALING = 1.0
        key = jax.random.key(seed)
        ks = jax.random.split(key, 8)
        std = 1.0 / D_IN ** 0.5
        x = jax.random.normal(ks[0], (B, T, D_IN), dtype=jnp.float32)
        idx = jax.random.randint(ks[1], (B,), 0, N_LORAS)
        gate = jax.nn.one_hot(idx, N_LORAS, dtype=jnp.float32)
        kernel = jax.random.normal(ks[2], (D_IN, D_OUT), dtype=jnp.float32) * std
        bias = jnp.zeros((D_OUT,), dtype=jnp.float32)
        lora_A = jax.random.normal(ks[3], (N_LORAS, RANK, D_IN), dtype=jnp.float32) * std
        lora_B = jax.random.normal(ks[4], (N_LORAS, D_OUT, RANK), dtype=jnp.float32) * 0.01
        lora_A_shared = jax.random.normal(ks[5], (RANK, D_IN), dtype=jnp.float32) * std
        lora_B_shared = jax.random.normal(ks[6], (D_OUT, RANK), dtype=jnp.float32) * 0.01
        return {'x': x, 'gate': gate, 'kernel': kernel, 'bias': bias, 'lora_A': lora_A, 'lora_B': lora_B, 'lora_A_shared': lora_A_shared, 'lora_B_shared': lora_B_shared}
    _L1_ffn_all = _L1_ffn_setup()
    _L1_ffn_in = {k: v for k, v in _L1_ffn_all.items() if k in ('gate', 'kernel', 'bias', 'lora_A', 'lora_B', 'lora_A_shared', 'lora_B_shared')}
    del _L1_ffn_all

    def _L2_cond_setup():
        import jax, jax.numpy as jnp
        import numpy as np
        MAX_LORAS, OUT, IN = (8, 512, 512)
        B, S = (4, 256)
        key = jax.random.key(seed)
        k1, k2, k3 = jax.random.split(key, 3)
        x = jax.random.normal(k1, (B, S, IN), dtype=jnp.float32)
        weight = jax.random.normal(k2, (MAX_LORAS, OUT, IN), dtype=jnp.float32) * 0.02
        adapter_ids = jax.random.randint(k3, (B,), 0, MAX_LORAS, dtype=jnp.int32)
        return {'x': x, 'weight': weight, 'adapter_ids': adapter_ids}
    _L2_cond_all = _L2_cond_setup()
    _L2_cond_in = {k: v for k, v in _L2_cond_all.items() if k in ('weight',)}
    del _L2_cond_all

    def _L2_ffn_setup():
        import jax, jax.numpy as jnp
        import numpy as np
        TOP_K = 2
        key = jax.random.key(seed)
        k1, k2, k3 = jax.random.split(key, 3)
        B, S, H, O, E = (32, 1, 512, 512, 8)
        x = jax.random.normal(k1, (B, S, H), dtype=jnp.float32)
        gate_w = jax.random.normal(k2, (H, E), dtype=jnp.float32) * 0.02
        expert_w = jax.random.normal(k3, (E, H, O), dtype=jnp.float32) * 0.02
        return {'x': x, 'gate_w': gate_w, 'expert_w': expert_w}
    _L2_ffn_all = _L2_ffn_setup()
    _L2_ffn_in = {k: v for k, v in _L2_ffn_all.items() if k in ('gate_w', 'expert_w')}
    del _L2_ffn_all

    def _L3_cond_setup():
        import jax, jax.numpy as jnp
        import numpy as np
        B, N, H, F = (4, 64, 512, 1376)
        L, R, RANK = (1, 16, 16)
        SCALE = 0.5
        key = jax.random.key(seed)
        ks = jax.random.split(key, 12)
        nrm = lambda k, shape, fan: jax.random.normal(k, shape, jnp.float32) * fan ** (-0.5)
        inp = {'x': jax.random.normal(ks[0], (B, N, H), jnp.float32), 'W_gate': nrm(ks[1], (F, H), H), 'W_up': nrm(ks[2], (F, H), H), 'W_down': nrm(ks[3], (H, F), F), 'A_gate': nrm(ks[4], (L, R, RANK, H), H), 'B_gate': nrm(ks[5], (L, R, F, RANK), RANK), 'A_up': nrm(ks[6], (L, R, RANK, H), H), 'B_up': nrm(ks[7], (L, R, F, RANK), RANK), 'A_down': nrm(ks[8], (L, R, RANK, F), F), 'B_down': nrm(ks[9], (L, R, H, RANK), RANK), 'lora_indices': jax.random.randint(ks[10], (B,), 0, R), 'layer_idx': 0}
        return inp
    _L3_cond_all = _L3_cond_setup()
    _L3_cond_in = {k: v for k, v in _L3_cond_all.items() if k in ('W_gate', 'W_up', 'W_down', 'A_gate', 'B_gate', 'A_up', 'B_up', 'A_down', 'B_down')}
    del _L3_cond_all

    def _L3_ffn_setup():
        import jax, jax.numpy as jnp
        import numpy as np
        SCALING = 16.0 / 8.0
        GAMMA = 1.0
        EPS = 1e-12
        key = jax.random.key(seed)
        ks = jax.random.split(key, 8)
        B, T, H, O = (4, 256, 512, 512)
        E_tot, E_act, r = (16, 4, 8)
        return {'x': jax.random.normal(ks[0], (B, T, H), jnp.float32), 'W_base': jax.random.normal(ks[1], (O, H), jnp.float32) * 0.02, 'b_base': jax.random.normal(ks[2], (O,), jnp.float32) * 0.02, 'lora_A': jax.random.normal(ks[3], (E_tot, r, H), jnp.float32) * 0.02, 'lora_B': jax.random.normal(ks[4], (E_tot, O, r), jnp.float32) * 0.02, 'router_W': jax.random.normal(ks[5], (E_tot, H), jnp.float32) * 0.02, 'router_b': jax.random.normal(ks[6], (E_tot,), jnp.float32) * 0.02, 'domain_prior': jax.random.uniform(ks[7], (E_tot,), jnp.float32), 'active': jnp.arange(E_act, dtype=jnp.int32)}
    _L3_ffn_all = _L3_ffn_setup()
    _L3_ffn_in = {k: v for k, v in _L3_ffn_all.items() if k in ('W_base', 'b_base', 'lora_A', 'lora_B', 'router_W', 'router_b', 'domain_prior', 'active')}
    del _L3_ffn_all
    return {'x': x, 'itok_Bx16_0_63': itok_Bx16_0_63, 'itok_B_207_1644': itok_B_207_1644, 'condB_coeff': condB_coeff, 'itok_B_3_7': itok_B_3_7, 'itok_B_2_6': itok_B_2_6, 'mask_Bx4096x4096_ik1': mask_Bx4096x4096_ik1, 'L0_cond_Wq': _L0_cond_in['Wq'], 'L0_cond_Wk': _L0_cond_in['Wk'], 'L0_cond_Wv': _L0_cond_in['Wv'], 'L0_cond_Wo': _L0_cond_in['Wo'], 'L0_cond_q_norm_w': _L0_cond_in['q_norm_w'], 'L0_cond_k_norm_w': _L0_cond_in['k_norm_w'], 'L0_cond_k_cache': _L0_cond_in['k_cache'], 'L0_cond_v_cache': _L0_cond_in['v_cache'], 'L0_ffn_weight_int8': _L0_ffn_in['weight_int8'], 'L0_ffn_scale': _L0_ffn_in['scale'], 'L0_ffn_bias': _L0_ffn_in['bias'], 'L1_cond_W': _L1_cond_in['W'], 'L1_cond_b': _L1_cond_in['b'], 'L1_ffn_gate': _L1_ffn_in['gate'], 'L1_ffn_kernel': _L1_ffn_in['kernel'], 'L1_ffn_bias': _L1_ffn_in['bias'], 'L1_ffn_lora_A': _L1_ffn_in['lora_A'], 'L1_ffn_lora_B': _L1_ffn_in['lora_B'], 'L1_ffn_lora_A_shared': _L1_ffn_in['lora_A_shared'], 'L1_ffn_lora_B_shared': _L1_ffn_in['lora_B_shared'], 'L2_cond_weight': _L2_cond_in['weight'], 'L2_ffn_gate_w': _L2_ffn_in['gate_w'], 'L2_ffn_expert_w': _L2_ffn_in['expert_w'], 'L3_cond_W_gate': _L3_cond_in['W_gate'], 'L3_cond_W_up': _L3_cond_in['W_up'], 'L3_cond_W_down': _L3_cond_in['W_down'], 'L3_cond_A_gate': _L3_cond_in['A_gate'], 'L3_cond_B_gate': _L3_cond_in['B_gate'], 'L3_cond_A_up': _L3_cond_in['A_up'], 'L3_cond_B_up': _L3_cond_in['B_up'], 'L3_cond_A_down': _L3_cond_in['A_down'], 'L3_cond_B_down': _L3_cond_in['B_down'], 'L3_ffn_W_base': _L3_ffn_in['W_base'], 'L3_ffn_b_base': _L3_ffn_in['b_base'], 'L3_ffn_lora_A': _L3_ffn_in['lora_A'], 'L3_ffn_lora_B': _L3_ffn_in['lora_B'], 'L3_ffn_router_W': _L3_ffn_in['router_W'], 'L3_ffn_router_b': _L3_ffn_in['router_b'], 'L3_ffn_domain_prior': _L3_ffn_in['domain_prior'], 'L3_ffn_active': _L3_ffn_in['active']}

def reference(x, itok_Bx16_0_63, itok_B_207_1644, condB_coeff, itok_B_3_7, itok_B_2_6, mask_Bx4096x4096_ik1, L0_cond_Wq, L0_cond_Wk, L0_cond_Wv, L0_cond_Wo, L0_cond_q_norm_w, L0_cond_k_norm_w, L0_cond_k_cache, L0_cond_v_cache, L0_ffn_weight_int8, L0_ffn_scale, L0_ffn_bias, L1_cond_W, L1_cond_b, L1_ffn_gate, L1_ffn_kernel, L1_ffn_bias, L1_ffn_lora_A, L1_ffn_lora_B, L1_ffn_lora_A_shared, L1_ffn_lora_B_shared, L2_cond_weight, L2_ffn_gate_w, L2_ffn_expert_w, L3_cond_W_gate, L3_cond_W_up, L3_cond_W_down, L3_cond_A_gate, L3_cond_B_gate, L3_cond_A_up, L3_cond_B_up, L3_cond_A_down, L3_cond_B_down, L3_ffn_W_base, L3_ffn_b_base, L3_ffn_lora_A, L3_ffn_lora_B, L3_ffn_router_W, L3_ffn_router_b, L3_ffn_domain_prior, L3_ffn_active):
    import jax
    import jax.numpy as jnp

    def _L0_cond_ref(x, Wq, Wk, Wv, Wo, q_norm_w, k_norm_w, k_cache, v_cache, block_table, cache_seqlens):
        import jax, jax.numpy as jnp
        import numpy as np
        B, S, HID = (4, 128, 512)
        D, HQ, HK = (128, 32, 8)
        PAGES, PSIZE, NPP = (64, 32, 16)
        THETA = 10000.0
        EPS = 1e-06
        SCALE = 1.0 / float(np.sqrt(D))

        def _rmsnorm(t, w):
            var = jnp.mean(t * t, axis=-1, keepdims=True)
            return t * jax.lax.rsqrt(var + EPS) * w

        def _rope(t, pos):
            inv_freq = 1.0 / THETA ** (jnp.arange(0, D, 2, dtype=jnp.float32) / D)
            freqs = pos[..., None].astype(jnp.float32) * inv_freq
            cos = jnp.cos(freqs)[:, :, None, :]
            sin = jnp.sin(freqs)[:, :, None, :]
            t1, t2 = (t[..., :D // 2], t[..., D // 2:])
            return jnp.concatenate([t1 * cos - t2 * sin, t2 * cos + t1 * sin], axis=-1)
        bsz, seqlen, _ = x.shape
        q = jnp.einsum('bsd,ed->bse', x, Wq).reshape(bsz, seqlen, HQ, D)
        k = jnp.einsum('bsd,ed->bse', x, Wk).reshape(bsz, seqlen, HK, D)
        v = jnp.einsum('bsd,ed->bse', x, Wv).reshape(bsz, seqlen, HK, D)
        q = _rmsnorm(q, q_norm_w)
        k = _rmsnorm(k, k_norm_w)
        pos = cache_seqlens[:, None] + jnp.arange(seqlen)[None, :]
        q = _rope(q, pos)
        k = _rope(k, pos)
        L = NPP * PSIZE
        kc = k_cache[block_table].reshape(bsz, L, HK, D)
        vc = v_cache[block_table].reshape(bsz, L, HK, D)
        k_all = jnp.concatenate([kc, k], axis=1)
        v_all = jnp.concatenate([vc, v], axis=1)
        valid_c = jnp.arange(L)[None, :] < cache_seqlens[:, None]
        valid = jnp.concatenate([valid_c, jnp.ones((bsz, seqlen), dtype=bool)], axis=1)
        rep = HQ // HK
        k_all = jnp.repeat(k_all, rep, axis=2)
        v_all = jnp.repeat(v_all, rep, axis=2)
        scores = jnp.einsum('bqhd,bkhd->bhqk', q, k_all) * SCALE
        scores = jnp.where(valid[:, None, None, :], scores, -1e+30)
        probs = jax.nn.softmax(scores, axis=-1)
        o = jnp.einsum('bhqk,bkhd->bqhd', probs, v_all)
        o = o.reshape(bsz, seqlen, HQ * D)
        return jnp.einsum('bse,de->bsd', o, Wo)

    def _L0_ffn_ref(x, weight_int8, scale, bias):
        import jax, jax.numpy as jnp
        import numpy as np
        B, S, D_IN, D_OUT = (4, 256, 512, 512)
        weight_fp = weight_int8.astype(x.dtype) * scale[:, None]
        out = jnp.einsum('bsd,od->bso', x, weight_fp) + bias
        return out

    def _L1_cond_ref(hidden_states, W, b, coeff, mask):
        import jax, jax.numpy as jnp
        import numpy as np
        B, S, D_IN, D_OUT = (4, 64, 512, 512)
        output = jnp.einsum('bsi,oi->bso', hidden_states, W) + b
        sign = (2 * mask - 1).astype(hidden_states.dtype)
        diff = jnp.einsum('bsi,bio->bso', hidden_states, sign)
        return output + diff * coeff[:, None, None]

    def _L1_ffn_ref(x, gate, kernel, bias, lora_A, lora_B, lora_A_shared, lora_B_shared):
        import jax, jax.numpy as jnp
        import numpy as np
        B, T, D_IN, D_OUT = (8, 256, 512, 512)
        N_LORAS, RANK = (16, 32)
        SCALING = 1.0
        base_out = jnp.matmul(x, kernel) + bias
        b = gate.shape[0]
        x_flat = x.reshape(b, -1, x.shape[-1])
        A_eff = jnp.einsum('bn,nri->bri', gate, lora_A)
        B_eff = jnp.einsum('bn,nor->bor', gate, lora_B)
        Ax = jnp.einsum('bri,bti->btr', A_eff, x_flat)
        delta_flat = jnp.einsum('bor,btr->bto', B_eff, Ax)
        Ax_s = jnp.einsum('ri,bti->btr', lora_A_shared, x_flat)
        delta_flat = delta_flat + jnp.einsum('or,btr->bto', lora_B_shared, Ax_s)
        delta = delta_flat.reshape(x.shape[:-1] + (kernel.shape[-1],))
        return base_out + (SCALING * delta).astype(base_out.dtype)

    def _L2_cond_ref(x, weight, adapter_ids):
        import jax, jax.numpy as jnp
        import numpy as np
        MAX_LORAS, OUT, IN = (8, 512, 512)
        B, S = (4, 256)
        w = weight[adapter_ids]
        return jnp.einsum('bsi,boi->bso', x, w)

    def _L2_ffn_ref(x, gate_w, expert_w):
        import jax, jax.numpy as jnp
        import numpy as np
        TOP_K = 2
        E = expert_w.shape[0]
        gate_logits = jnp.einsum('bsh,he->bse', x, gate_w)
        top_vals, top_idx = jax.lax.top_k(gate_logits, TOP_K)
        probs = jax.nn.softmax(top_vals, axis=-1)
        onehot = jax.nn.one_hot(top_idx, E, dtype=x.dtype)
        w_e = jnp.einsum('bsk,bske->bse', probs, onehot)
        expert_out = jnp.einsum('bsh,eho->bseo', x, expert_w)
        out = jnp.einsum('bseo,bse->bso', expert_out, w_e)
        return out

    def _L3_cond_ref(x, W_gate, W_up, W_down, A_gate, B_gate, A_up, B_up, A_down, B_down, lora_indices, layer_idx):
        import jax, jax.numpy as jnp
        import numpy as np
        B, N, H, F = (4, 64, 512, 1376)
        L, R, RANK = (1, 16, 16)
        SCALE = 0.5

        def lora_add(base, inp, A, B):
            Ab = A[layer_idx][lora_indices]
            Bb = B[layer_idx][lora_indices]
            t = jnp.einsum('bri,bni->bnr', Ab, inp)
            return base + jnp.einsum('bor,bnr->bno', Bb, t) * SCALE
        gate = lora_add(jnp.einsum('bnh,fh->bnf', x, W_gate), x, A_gate, B_gate)
        up = lora_add(jnp.einsum('bnh,fh->bnf', x, W_up), x, A_up, B_up)
        act = jax.nn.silu(gate) * up
        down = lora_add(jnp.einsum('bnf,hf->bnh', act, W_down), act, A_down, B_down)
        return down

    def _L3_ffn_ref(x, W_base, b_base, lora_A, lora_B, router_W, router_b, domain_prior, active):
        import jax, jax.numpy as jnp
        import numpy as np
        SCALING = 16.0 / 8.0
        GAMMA = 1.0
        EPS = 1e-12
        y = jnp.einsum('bth,oh->bto', x, W_base) + b_base
        A = lora_A[active]
        Bm = lora_B[active]
        z = jnp.einsum('bth,erh->bter', x, A)
        contribs = jnp.einsum('bter,eor->bteo', z, Bm) * SCALING
        logits = jnp.einsum('bth,eh->bte', x, router_W) + router_b
        logits = logits[..., active]
        prior = domain_prior[active]
        alpha = jax.nn.softmax(jnp.log(prior + EPS) + logits / GAMMA, axis=-1)
        return y + jnp.einsum('bteo,bte->bto', contribs, alpha)
    x = x + _L0_ffn_ref(_L0_cond_ref(x, L0_cond_Wq, L0_cond_Wk, L0_cond_Wv, L0_cond_Wo, L0_cond_q_norm_w, L0_cond_k_norm_w, L0_cond_k_cache, L0_cond_v_cache, itok_Bx16_0_63, itok_B_207_1644), L0_ffn_weight_int8, L0_ffn_scale, L0_ffn_bias)
    x = x + _L1_ffn_ref(_L1_cond_ref(x, L1_cond_W, L1_cond_b, condB_coeff, mask_Bx4096x4096_ik1), L1_ffn_gate, L1_ffn_kernel, L1_ffn_bias, L1_ffn_lora_A, L1_ffn_lora_B, L1_ffn_lora_A_shared, L1_ffn_lora_B_shared)
    x = x + _L2_ffn_ref(_L2_cond_ref(x, L2_cond_weight, itok_B_3_7), L2_ffn_gate_w, L2_ffn_expert_w)
    x = x + _L3_ffn_ref(_L3_cond_ref(x, L3_cond_W_gate, L3_cond_W_up, L3_cond_W_down, L3_cond_A_gate, L3_cond_B_gate, L3_cond_A_up, L3_cond_B_up, L3_cond_A_down, L3_cond_B_down, itok_B_2_6, 0), L3_ffn_W_base, L3_ffn_b_base, L3_ffn_lora_A, L3_ffn_lora_B, L3_ffn_router_W, L3_ffn_router_b, L3_ffn_domain_prior, L3_ffn_active)
    return x

_drawn_inputs = setup_inputs


def setup_inputs(seed=0):
    import zlib

    import numpy as np

    out = dict(_drawn_inputs(seed))
    spreads = {'L1_ffn_bias': (0.0, 0.1)}
    factors = {'L0_cond_k_norm_w': 3.781,
     'L1_cond_b': 4.088,
     'L3_ffn_b_base': 8.0,
     'L3_ffn_router_b': 64.0,
     'L3_ffn_domain_prior': 19.681}
    for name, (base, spread) in spreads.items():
        noise = np.random.default_rng([zlib.crc32(name.encode()), seed]).standard_normal(out[name].shape)
        drawn = base * np.exp(spread * noise) if base else spread * noise
        out[name] = jnp.asarray(drawn.astype(out[name].dtype))
    for name, factor in factors.items():
        out[name] = (out[name] * factor).astype(out[name].dtype)
    return out
```

```python
from contextlib import ExitStack

import numpy as np
import concourse.bass as bass
from concourse import mybir

F32 = mybir.dt.float32
F32R = mybir.dt.float32r
I32 = mybir.dt.int32
ALU = mybir.AluOpType
ACT = mybir.ActivationFunctionType
AX = mybir.AxisListType

P = 128
NB, D_MODEL = 8, 512
CH = D_MODEL // P
HQ, HK = 32, 8
REP = HQ // HK
PAGES, PSIZE, NPP = 64, 32, 16
CACHE = NPP * PSIZE
KEYS = CACHE + P
KB = KEYS // P
KBC = CACHE // P
STEPS = HK * NB
SCALE = 1.0 / float(np.sqrt(P))
RMS_EPS = 1e-6
MASKED = -1e30

WQ0, WKV0, WO0 = 0, CH * REP * P, CH * REP * P + CH * 2 * P
WCOLS = WO0 + REP * D_MODEL
PIECE = WCOLS // NB
AHEAD = 10
LAST_SPLIT = STEPS - AHEAD - 1

PS_S = 0
PS_V, PS_K, PS_Q = 1280, 1408, 1536
PS_RING = (2048, 2560)
PS_O, PS_Y = 3072, 3584

PARTS = ((0, 0), (0, 1), (1, 0))


def need(eng, sem, value):
    if not isinstance(value, int) or value > 0:
        eng.wait_ge(sem, value)


def plain(eng):
    eng.nop(nofuse=True)


class Semaphores:

    def __init__(self, nc):
        self.nc, self.handles = nc, []

    def new(self, name):
        self.handles.append(self.nc.alloc_semaphore(name=name))
        return self.handles[-1]

    def release(self):
        self.nc.clear_and_free_semaphores(self.handles)
        self.nc.all_engine_barrier()


def fills_before(s):
    if isinstance(s, int):
        if s <= 0:
            return 0 if s < 0 else 3
        if s == STEPS:
            return 8 * s - 2 - 3
    return s * 8 - 2


def stages(s):
    if not isinstance(s, int):
        return True, True, True, True
    return s + 1 < STEPS, 0 <= s < STEPS, 1 <= s <= STEPS, 2 <= s <= STEPS + 1


def over_steps(eng, step):
    for s in (-1, 0, 1):
        step(s, s % 2, True)
    with eng.Fori(2, LAST_SPLIT, 2) as s:
        step(s, 0, True)
        step(s + 1, 1, True)
    with eng.Fori(LAST_SPLIT + 1, STEPS - 3, 2) as s:
        step(s, 0, False)
        step(s + 1, 1, False)
    for s in range(STEPS - 2, STEPS + 2):
        step(s, s % 2, False)


def attention(nc, ctx, sems, io, ident, y):
    def sb(name, shape, dt=F32):
        return ctx.enter_context(nc.sbuf_tensor(f"att_{name}", shape, dt))

    def sem(name):
        return sems.new(f"att_{name}")

    def pair(name):
        return [sem(f"{name}{i}") for i in range(2)]

    x_scr = nc.dram_tensor("x_scr", (NB, P, 2 * D_MODEL), F32, kind="Internal").ap()
    tab_scr = nc.dram_tensor("tab_scr", (NB, P, 4 * P), F32, kind="Internal").ap()
    mask_scr = nc.dram_tensor("mask_scr", (NB, KEYS), F32, kind="Internal").ap()
    k_rows = io["k_cache"].rearrange("p r h d -> (p r h) d")
    v_rows = io["v_cache"].rearrange("p r h d -> (p r h) d")

    ps = ctx.enter_context(nc.psum_tensor("att_ps", [P, 4096], F32))
    w = sb("w", [P, 2, 2, WCOLS], F32R)
    w_cols = w[:, :, :, :].rearrange("p a b c -> p (a b c)")
    prob = sb("prob", [P, 2, REP, KEYS])
    v = sb("v", [P, 2, 2, KB, P], F32R)
    kt = sb("kt", [P, 2, KEYS], F32R)
    qt = sb("qt", [P, 2, REP * P], F32R)
    pt = sb("pt", [P, 2, 2, REP * P], F32R)
    ot = sb("ot", [P, 2, REP * P], F32R)
    sq = sb("sq", [P, REP + 1, P])
    ra = sb("ra", [P, REP + 1, P])
    rb = sb("rb", [P, REP + 1, P])
    rc = sb("rc", [P, REP + 1, P])
    k_raw = sb("k_raw", [P, 2, KBC, P])
    v_raw = sb("v_raw", [P, 2, KBC, P])
    x_pk = sb("x_pk", [P, 2, 2, CH, P], F32R)
    tab = sb("tab", [P, 2, 4, P])
    mask = sb("mask", [P, 2, KEYS])
    w_raw = sb("w_raw", [P, 2, PIECE])
    ms = sb("ms", [P, 8])
    ms_eps = sb("ms_eps", [P, 8])
    power = sb("power", [P, 8])
    rinv = sb("rinv", [P, 8])
    top = sb("top", [P, 2, REP])
    neg = sb("neg", [P, 2, REP])
    total = sb("total", [P, 2, REP])
    inv = sb("inv", [P, 2, REP])
    idx_all = sb("idx_all", [P, STEPS, KBC], I32)
    idx_k = sb("idx_k", [P, 2, KBC], I32)
    idx_v = sb("idx_v", [P, 2, KBC], I32)
    table_sb = sb("table_sb", [P, NB, KBC], I32)
    len_i = sb("len_i", [P, NB], I32)
    pos = sb("pos", [P, NB])
    len_col = sb("len_col", [NB, 2], I32)
    len_f = sb("len_f", [NB, 2])
    tok = sb("tok", [P, 2])

    load, scr_x, scr_tab, scr_mask = sem("load"), sem("scr_x"), sem("scr_tab"), sem("scr_mask")
    first_w, w8 = sem("first_w"), sem("w8")
    pk_land, mask_land, w_land = pair("pk_land"), pair("mask_land"), pair("w_land")
    k_land, v_land = pair("k_land"), pair("v_land")
    pool_pre, act_pre, dve_link, idx_sem, angles, tab_part, piece8 = (
        sem(n) for n in ("pool_pre", "act_pre", "dve_link", "idx_sem", "angles", "tab_part", "piece8"))
    x_split, tab_done, w0_split, mask_done, y_zero = (sem(n) for n in ("x_split", "tab_done", "w0_split", "mask_done", "y_zero"))
    pe_q, pe_kv, pe_s, pe_fill, pe_pv, pe_wo = (sem(n) for n in ("pe_q", "pe_kv", "pe_s", "pe_fill", "pe_pv", "pe_wo"))
    act_sq, act_hi, act_exp, act_ot, act_vn, act_vc, act_w = (
        sem(n) for n in ("act_sq", "act_hi", "act_exp", "act_ot", "act_vn", "act_vc", "act_w"))
    dve_ms, dve_rope, dve_max, dve_neg, dve_lo, dve_inv, dve_norm, dve_ot, dve_vn, dve_vc, dve_w, dve_y = (
        sem(n) for n in ("dve_ms", "dve_rope", "dve_max", "dve_neg", "dve_lo", "dve_inv", "dve_norm", "dve_ot", "dve_vn", "dve_vc",
                         "dve_w", "dve_y"))
    pool_ms, pool_r, pool_sum, pool_rope, pool_idx = (sem(n) for n in ("pool_ms", "pool_r", "pool_sum", "pool_rope", "pool_idx"))

    x_raw = prob[:, :, :, :].rearrange("p a h k -> p (a h k)")[:, 0:NB * D_MODEL]
    w0_raw = prob[:, :, :, :].rearrange("p a h k -> p (a h k)")
    x_stage = w[:, 1, :, :].rearrange("p a c -> p (a c)")[:, 0:NB * 2 * D_MODEL].rearrange(
        "p (b a n) -> p b a n", b=NB, a=2)
    tables = y[:, :].rearrange("p (b f n) -> p b f n", b=NB, f=4)

    def flat(t, n=NB * P // 2):
        return t[:, :, :].rearrange("p a b -> p (a b)")[:, 0:n]

    block = ctx.enter_context(nc.Block())

    @block.sync
    def _(sp):
        sp.dma_start(x_raw, io["xT"]).then_inc(load, 16)
        sp.dma_start(len_i[:, :], io["lens"].rearrange("(a b) -> a b", a=1).to_broadcast([P, NB])).then_inc(load, 16)
        sp.dma_start(len_col[:, 0:1], io["lens"].rearrange("(b a) -> b a", a=1)).then_inc(load, 16)
        with nc.allow_non_contiguous_dma(reason="page numbers, a few words"):
            for r in range(P // PSIZE):
                sp.dma_start(table_sb[r * PSIZE:(r + 1) * PSIZE, :, :],
                             io["block_table"].rearrange("b (k r) -> r b k", r=P // PSIZE)[r:r + 1].to_broadcast(
                                 [PSIZE, NB, KBC])).then_inc(load, 16)
        sp.dma_start(w_raw[:, 0, 0:P // 2], io["inv_freq"].rearrange("(a b) -> a b", a=1).to_broadcast([P, P // 2])).then_inc(load, 16)
        sp.dma_start(w_raw[:, 0, P:2 * P], io["k_norm"].rearrange("(a b) -> a b", a=1).to_broadcast([P, P])).then_inc(load, 16)
        sp.dma_start(w_raw[:, 0, 2 * P:3 * P], io["q_norm"].rearrange("(a b) -> a b", a=1).to_broadcast([P, P])).then_inc(load, 16)
        sp.wait_ge(x_split, 2)
        sp.dma_start(w0_raw.rearrange("p (n c) -> p n c", n=NB), io["w_all"][0:NB].rearrange("n p c -> p n c")).then_inc(first_w, 16)
        sp.dma_start(x_scr.rearrange("b p n -> p b n"), x_stage.rearrange("p b a n -> p b (a n)").bitcast(F32)).then_inc(scr_x, 16)
        sp.wait_ge(mask_done, 2)
        sp.dma_start(mask_scr, sq[0:NB, :, :].rearrange("p a b -> p (a b)")).then_inc(scr_mask, 16)
        sp.wait_ge(tab_done, 4)
        sp.dma_start(tab_scr.rearrange("b p n -> p b n"), tables.rearrange("p b f n -> p b (f n)")).then_inc(scr_tab, 16)
        sp.dma_start(w_raw[:, 0, :], io["w_all"][NB]).then_inc(w8, 16)
        sp.dma_start(w_raw[:, 1, :], io["w_all"][NB + 1]).then_inc(w_land[1], 16)
        sp.wait_ge(scr_x, 16)
        sp.wait_ge(scr_tab, 16)
        sp.wait_ge(scr_mask, 16)

        def packet(t, p):
            sp.dma_start(x_pk[:, p, :, :, :].bitcast(F32), x_scr[bass.ds(t % NB, 1)].rearrange("a p n -> p (a n)")
                         if not isinstance(t, int) else x_scr[t % NB]).then_inc(pk_land[p], 16)

        def packet_tab(t, p):
            sp.dma_start(tab[:, p, :, :], tab_scr[bass.ds(t % NB, 1)].rearrange("a p n -> p (a n)")
                         if not isinstance(t, int) else tab_scr[t % NB]).then_inc(pk_land[p], 16)

        def packet_mask(t, p):
            row = mask_scr[bass.ds(t % NB, 1)] if not isinstance(t, int) else mask_scr[t % NB:t % NB + 1]
            sp.dma_start(mask[:, p, :], row.to_broadcast([P, KEYS])).then_inc(mask_land[p], 16)

        def piece(n, p):
            src = io["w_all"][n] if isinstance(n, int) else io["w_all"][bass.ds(n, 1)].rearrange("a p n -> p (a n)")
            sp.dma_start(w_raw[:, p, :], src).then_inc(w_land[p], 16)

        for t in range(2):
            packet(t, t)
            packet_tab(t, t)
            packet_mask(t, t)
        sp.wait_ge(piece8, 1)
        piece(AHEAD, 0)

        def step(s, p, split):
            q = 1 - p
            more = not isinstance(s, int) or s + 3 < STEPS
            if more:
                sp.wait_ge(pe_q, s + 2)
                sp.wait_ge(pe_kv, s + 2)
                packet(s + 3, q)
                sp.wait_ge(dve_rope, s + 2)
                packet_tab(s + 3, q)
            if not isinstance(s, int) or 0 <= s < STEPS - 2:
                sp.wait_ge(dve_max, s * 4 + 4)
                packet_mask(s + 2, p)
            if split and (not isinstance(s, int) or s + AHEAD + 2 < STEPS):
                sp.wait_ge(act_w, s + 2)
                sp.wait_ge(dve_w, s + 2)
                piece(s + AHEAD + 2, p)

        for s in (-1, 0, 1):
            step(s, s % 2, True)
        with sp.Fori(2, LAST_SPLIT - 2, 2) as s:
            step(s, 0, True)
            step(s + 1, 1, True)
        with sp.Fori(LAST_SPLIT - 1, STEPS - 5, 2) as s:
            step(s, 0, False)
            step(s + 1, 1, False)
        for s in range(STEPS - 4, STEPS):
            step(s, s % 2, False)

    @block.gpsimd
    def _(pool):
        made = [0]

        def const(ins):
            made[0] += 1
            ins.then_inc(pool_pre, 1)
            pool.wait_ge(pool_pre, made[0])

        const(pool.memset(ident[:, :], 0.0))
        const(pool.memset(power[:, :], -0.5))
        const(pool.iota(tok[:, 0:1], [[0, 1]], base=0, channel_multiplier=1, allow_small_or_imprecise_dtypes=True))
        const(pool.iota(rc[0:NB, 0:KBC, :], [[P, KBC], [1, P]], base=0, channel_multiplier=0, allow_small_or_imprecise_dtypes=True))
        for r in range(P // PSIZE):
            const(pool.iota(idx_k[r * PSIZE:(r + 1) * PSIZE, 0, 0:1], [[0, 1]], base=0, channel_multiplier=HK))
        pool.affine_select(out=ident[:, :], in_=ident[:, :], compare_op=ALU.not_equal, fill=1.0, base=0,
                           pattern=[[-1, P]], channel_multiplier=1).then_inc(pool_pre, 1)

        def start_gather(rows, raw, idx, t, p, landed, count):
            cols = idx_all[:, t, :] if isinstance(t, int) else idx_all[:, bass.ds(t, 1), :].rearrange("p a k -> p (a k)")
            plain(pool)
            pool.tensor_copy(idx[:, p, :], cols).then_inc(pool_idx, 1)
            pool.wait_ge(pool_idx, count)
            plain(pool)
            for k in range(KBC):
                pool.indirect_dma_start(out=raw[:, p, k, :], out_offset=None, in_=rows,
                                        in_offset=bass.IndirectOffsetOnAxis(ap=idx[:, p, k:k + 1], axis=0)).then_inc(landed[p], 16)

        pool.wait_ge(idx_sem, HK)
        start_gather(k_rows, k_raw, idx_k, 0, 0, k_land, 1)

        def step(s, p, split):
            a, _, _, _ = stages(s)
            q = 1 - p
            if a:
                pool.wait_ge(dve_ms, s + 2)
                plain(pool)
                pool.tensor_scalar(ms_eps[:, 0:REP + 1], ms[:, 0:REP + 1], 1.0 / P, RMS_EPS, ALU.mult, ALU.add).then_inc(pool_ms, 1)
                pool.wait_ge(pool_ms, s + 2)
                pool.tensor_tensor(rinv[:, 0:REP + 1], ms_eps[:, 0:REP + 1], power[:, 0:REP + 1], ALU.pow).then_inc(pool_r, 1)
                pool.wait_ge(dve_rope, s + 2)
                need(pool, pe_fill, fills_before(s))
                pool.tensor_tensor(rc[:, :, :], ra[:, :, :], rb[:, :, :], ALU.add).then_inc(pool_sum, 1)
                pool.wait_ge(pool_r, s + 2)
                pool.wait_ge(pool_sum, s + 2)
                pool.tensor_tensor(rc[:, :, :], rc[:, :, :], rinv[:, 0:REP + 1].unsqueeze(2).to_broadcast([P, REP + 1, P]),
                                   ALU.mult).then_inc(pool_rope, 1)
            if not isinstance(s, int) or s + 2 < STEPS:
                if not isinstance(s, int) or s >= 0:
                    pool.wait_ge(k_land[p], (s - p) * 32 + 64)
                start_gather(k_rows, k_raw, idx_k, s + 2, p, k_land, s * 2 + 4)
            if a:
                if not isinstance(s, int) or s >= 1:
                    pool.wait_ge(v_land[q], (s - p) * 32 + (64 if p else 0))
                    pool.wait_ge(act_vc, s)
                    pool.wait_ge(dve_vc, s)
                start_gather(v_rows, v_raw, idx_v, s + 1, q, v_land, s * 2 + 5 if not isinstance(s, int) or s + 2 < STEPS else s * 2 + 4)

        over_steps(pool, step)

    @block.tensor
    def _(pe):
        def gcol(t, part, col, n):
            if isinstance(t, int):
                c = ((t // NB) % 2 * 2 + part) * WCOLS + col
                return w_cols[:, c:c + n]
            return w_cols[:, bass.ds((t // NB) % 2 * (2 * WCOLS) + part * WCOLS + col, n)]

        pe.wait_ge(w0_split, 2)
        pe.wait_ge(pool_pre, 5 + P // PSIZE)

        def project(t, p, col, n, out):
            for i, (a, b) in enumerate(PARTS):
                for c in range(CH):
                    mm = pe.matmul(ps[:, out:out + n], x_pk[:, p, a, c, :], gcol(t, b, col + c * n, n),
                                   start=(i == 0 and c == 0), stop=(i == 2 and c == CH - 1))
            return mm

        def scores(h):
            base = PS_S
            for lo, hi in ((0, CACHE), (CACHE, KEYS)):
                for i, (a, b) in enumerate(PARTS):
                    mm = pe.matmul(ps[:, base + lo:base + hi], qt[:, a, h * P:(h + 1) * P], kt[:, b, lo:hi],
                                   start=(i == 0), stop=(i == 2))
            return mm

        def values(p, k):
            for i, (a, b) in enumerate(PARTS):
                mm = pe.matmul(ps[:, PS_O:PS_O + REP * P], v[:, p, a, k, :], pt[:, k % 2, b, :],
                               start=(k == 0 and i == 0), stop=(k == KB - 1 and i == 2))
            return mm

        def step(s, p, split):
            a, sc, pv, wo = stages(s)
            q = 1 - p
            fills = fills_before(s)
            if not isinstance(s, int) or s >= 3:
                pe.wait_ge(dve_w, s - 1 if split or (isinstance(s, int) and s < LAST_SPLIT) else LAST_SPLIT + 2)
            if a:
                pe.wait_ge(pk_land[q], (s + 1 - q) * 16 + 32)
                need(pe, dve_rope, s + 1)
                need(pe, act_sq, s + 1)
                project(s + 1, q, WQ0, REP * P, PS_Q).then_inc(pe_q, 1)
                need(pe, dve_vn, s + 1)
                project(s + 1, q, WKV0, 2 * P, PS_V).then_inc(pe_kv, 1)
            if wo:
                pe.wait_ge(dve_ot, s - 1)
                need(pe, dve_y, s - 2)
                for i, (x, b) in enumerate(PARTS):
                    for h in range(REP):
                        mm = pe.matmul(ps[:, PS_Y:PS_Y + D_MODEL], ot[:, x, h * P:(h + 1) * P],
                                       gcol(s - 2, b, WO0 + h * D_MODEL, D_MODEL),
                                       start=(i == 0 and h == 0), stop=(i == 2 and h == REP - 1))
                mm.then_inc(pe_wo, 1)

            def one_scores(h):
                need(pe, dve_max, s * 4 + h)
                scores(h).then_inc(pe_s, 1)

            def ring_free(n, first=False):
                need(pe, dve_lo, fills + n if first else fills + (n - 1))

            def turn_probs(k):
                ring_free(k, first=(isinstance(s, int) and s == STEPS and k == 0))
                for h in range(REP):
                    mm = pe.transpose(ps[:, PS_RING[k % 2] + h * P:PS_RING[k % 2] + (h + 1) * P],
                                      prob[:, q, h, k * P:(k + 1) * P], ident[:, :])
                mm.then_inc(pe_fill, 1)

            def one_values(k):
                pe.wait_ge(dve_lo, fills + (k + 1))
                values(q, k).then_inc(pe_pv, 1)

            if sc:
                pe.wait_ge(dve_lo, fills)
                one_scores(0)
            if pv:
                pe.wait_ge(dve_norm, s)
                turn_probs(0)
            if sc:
                one_scores(1)
            if pv:
                turn_probs(1)
                pe.wait_ge(dve_vc, s)
                pe.wait_ge(dve_vn, s)
                one_values(0)
            if sc:
                one_scores(2)
            if pv:
                turn_probs(2)
                one_values(1)
            if sc:
                one_scores(3)
            if pv:
                turn_probs(3)
                one_values(2)
                turn_probs(4)
                one_values(3)
            n = KB if pv else 0
            if a:
                pe.wait_ge(k_land[q], (s + 1 - q) * 32 + 64)
                ring_free(n, first=(isinstance(s, int) and s == 0))
                for k in range(KBC):
                    mm = pe.transpose(ps[:, PS_RING[1] + k * P:PS_RING[1] + (k + 1) * P], k_raw[:, q, k, :], ident[:, :])
                mm.then_inc(pe_fill, 1)
            if pv:
                one_values(4)
            if a:
                pe.wait_ge(pool_rope, s + 2)
                ring_free(n + 1)
                for h in range(REP):
                    mm = pe.transpose(ps[:, PS_RING[0] + h * P:PS_RING[0] + (h + 1) * P], rc[:, 1 + h, :], ident[:, :])
                mm.then_inc(pe_fill, 1)
                ring_free(n + 2)
                pe.transpose(ps[:, PS_RING[1]:PS_RING[1] + P], rc[:, 0, :], ident[:, :]).then_inc(pe_fill, 1)

        over_steps(pe, step)

    @block.scalar
    def _(act):
        act.wait_ge(angles, 1)
        act.activation(flat(ra), flat(ra), ACT.Sin).then_inc(act_pre, 1)
        act.activation(flat(rb), flat(rb), ACT.Sin).then_inc(act_pre, 1)
        act.wait_ge(w0_split, 2)

        def hi(out, src, done):
            act.activation(out, src, ACT.Copy).then_inc(done, 1)

        def gcol_piece(n, part):
            if isinstance(n, int):
                c = ((n // NB) % 2 * 2 + part) * WCOLS + (n % NB) * PIECE
                return w_cols[:, c:c + PIECE]
            return w_cols[:, bass.ds((n // NB) % 2 * (2 * WCOLS) + (n % NB) * PIECE + part * WCOLS, PIECE)]

        def step(s, p, split):
            a, sc, pv, wo = stages(s)
            q = 1 - p
            fills = fills_before(s)
            if a:
                act.wait_ge(pe_q, s + 2)
                act.wait_ge(pe_kv, s + 2)
                need(act, dve_ms, s + 1)
                act.activation(sq[:, :, :], ps[:, PS_K:PS_K + (REP + 1) * P], ACT.Square).then_inc(act_sq, 1)

            def exp(h):
                act.wait_ge(dve_neg, s * 4 + (h + 1))
                act.activation(prob[:, p, h, :], prob[:, p, h, :], ACT.Exp, bias=neg[:, p, h:h + 1], scale=SCALE,
                               accum_out=total[:, p, h:h + 1]).then_inc(act_exp, 1)

            for k in range(KB):
                if pv:
                    act.wait_ge(pe_fill, fills + (k + 1))
                    if k >= 2:
                        act.wait_ge(pe_pv, s * 5 + (k - 6))
                    else:
                        need(act, pe_pv, s * 5 - 5 if k == 0 else (s * 5 - 6))
                    hi(pt[:, k % 2, 0, :], ps[:, PS_RING[k % 2]:PS_RING[k % 2] + REP * P], act_hi)
                if sc and k < REP:
                    exp(k)
            n = KB if pv else 0
            if a:
                act.wait_ge(pe_fill, fills + (n + 1))
                hi(kt[:, 0, 0:CACHE], ps[:, PS_RING[1]:PS_RING[1] + CACHE], act_hi)
            if pv:
                act.wait_ge(pe_pv, s * 5)
                hi(ot[:, 0, :], ps[:, PS_O:PS_O + REP * P], act_ot)
            if a:
                act.wait_ge(pe_fill, fills + (n + 2))
                hi(qt[:, 0, :], ps[:, PS_RING[0]:PS_RING[0] + REP * P], act_hi)
                act.wait_ge(pe_fill, fills + (n + 3))
                hi(kt[:, 0, CACHE:KEYS], ps[:, PS_RING[1]:PS_RING[1] + P], act_hi)
                act.wait_ge(dve_rope, s + 2)
                hi(v[:, q, 0, KBC, :], ps[:, PS_V:PS_V + P], act_vn)
            if sc:
                act.wait_ge(v_land[p], (s - p) * 32 + 64)
                hi(v[:, p, 0, 0:KBC, :], v_raw[:, p, :, :], act_vc)
            if split:
                act.wait_ge(w_land[p], (s - p) * 8 + 16 + (0 if p == 0 else 16))
                hi(gcol_piece(s + AHEAD, 0), w_raw[:, p, :], act_w)

        over_steps(act, step)

    @block.vector
    def _(dve):
        chain = [0]

        def link(ins):
            chain[0] += 1
            ins.then_inc(dve_link, 1)
            dve.wait_ge(dve_link, chain[0])

        dve.wait_ge(load, 16 * (3 + P // PSIZE + 3))
        dve.wait_ge(pool_pre, 4 + P // PSIZE)
        xr = x_raw.rearrange("p (b n) -> p b n", b=NB)
        dve.tensor_copy(x_stage[:, :, 0, :], xr).then_inc(x_split, 1)
        dve.wait_ge(x_split, 1)
        dve.tensor_tensor(x_stage[:, :, 1, :], xr, x_stage[:, :, 0, :].bitcast(F32), ALU.subtract).then_inc(x_split, 1)
        tf = flat(rb, NB * KBC).rearrange("p (b k) -> p b k", b=NB)
        link(dve.tensor_copy(tf, table_sb[:, :, :]))
        link(dve.tensor_copy(tok[:, 1:2], idx_k[:, 0, 0:1]))
        link(dve.tensor_scalar(tf, tf, float(PSIZE * HK), tok[:, 1:2], ALU.mult, ALU.add))
        for g in range(HK):
            dve.tensor_scalar(idx_all[:, g * NB:(g + 1) * NB, :], tf, float(g), None, ALU.add).then_inc(idx_sem, 1)
        link(dve.memset(sq[0:NB, :, :], 0.0))
        link(dve.tensor_copy(len_f[:, 0:1], len_col[:, 0:1]))
        dve.tensor_scalar(sq[0:NB, 0:KBC, :], rc[0:NB, 0:KBC, :], len_f[:, 0:1], MASKED, ALU.is_ge, ALU.mult).then_inc(mask_done, 2)
        link(dve.tensor_copy(pos[:, :], len_i[:, :]))
        link(dve.tensor_scalar(pos[:, :], pos[:, :], tok[:, 0:1], None, ALU.add))
        half = P // 2
        theta = flat(ra).rearrange("p (b n) -> p b n", b=NB)
        turns = flat(rc)
        dve.wait_ge(mask_done, 2)
        dve.wait_ge(idx_sem, HK)
        link(dve.tensor_tensor(theta, pos[:, :].unsqueeze(2).to_broadcast([P, NB, half]),
                               w_raw[:, 0, 0:half].rearrange("p (a n) -> p a n", a=1).to_broadcast([P, NB, half]), ALU.mult))
        two_pi = 2.0 * np.pi
        c1 = 6.28125
        c2 = float(np.float32(np.round((two_pi - c1) * 2.0 ** 22) / 2.0 ** 22))
        c3 = float(np.float32(two_pi - c1 - c2))
        magic = 1.5 * 2.0 ** 23
        link(dve.tensor_scalar(turns, flat(ra), float(1.0 / two_pi), magic, ALU.mult, ALU.add))
        link(dve.tensor_scalar(turns, turns, -magic, None, ALU.add))
        for c in (c1, c2, c3):
            link(dve.scalar_tensor_tensor(out=flat(ra), in0=turns, scalar=-c, in1=flat(ra), op0=ALU.mult, op1=ALU.add))
        lim = 3.1415925
        link(dve.tensor_scalar(turns, flat(ra), float(np.pi / 2), -two_pi, ALU.is_gt, ALU.mult))
        link(dve.scalar_tensor_tensor(out=flat(rb), in0=flat(ra), scalar=float(np.pi / 2), in1=turns, op0=ALU.add, op1=ALU.add))
        link(dve.tensor_scalar(flat(rb), flat(rb), lim, -lim, ALU.min, ALU.max))
        dve.tensor_scalar(flat(ra), flat(ra), lim, -lim, ALU.min, ALU.max).then_inc(angles, 1)
        dve.wait_ge(act_pre, 2)
        sin = flat(ra).rearrange("p (b n) -> p b n", b=NB)
        cos = flat(rb).rearrange("p (b n) -> p b n", b=NB)
        for i, col in ((0, P), (2, 2 * P)):
            w1 = w_raw[:, 0, col:col + half].rearrange("p (a n) -> p a n", a=1).to_broadcast([P, NB, half])
            w2 = w_raw[:, 0, col + half:col + P].rearrange("p (a n) -> p a n", a=1).to_broadcast([P, NB, half])
            dve.tensor_tensor(tables[:, :, i, 0:half], cos, w1, ALU.mult).then_inc(tab_part, 1)
            dve.tensor_tensor(tables[:, :, i, half:P], cos, w2, ALU.mult).then_inc(tab_part, 1)
            dve.tensor_tensor(tables[:, :, i + 1, 0:half], sin, w2, ALU.mult).then_inc(tab_part, 1)
            dve.tensor_tensor(tables[:, :, i + 1, half:P], sin, w1, ALU.mult).then_inc(tab_part, 1)
        dve.wait_ge(tab_part, 8)
        for i in (1, 3):
            dve.tensor_scalar(tables[:, :, i, 0:half], tables[:, :, i, 0:half], -1.0, None, ALU.mult).then_inc(tab_done, 2)
        dve.wait_ge(first_w, 16)
        dve.tensor_copy(w[:, 0, 0, :], w0_raw).then_inc(w0_split, 1)
        dve.wait_ge(w0_split, 1)
        dve.tensor_tensor(w[:, 0, 1, :], w0_raw, w[:, 0, 0, :].bitcast(F32), ALU.subtract).then_inc(w0_split, 1)
        dve.wait_ge(w8, 16)
        dve.wait_ge(scr_x, 16)
        link(dve.tensor_copy(w[:, 1, 0, 0:PIECE], w_raw[:, 0, :]))
        dve.tensor_tensor(w[:, 1, 1, 0:PIECE], w_raw[:, 0, :], w[:, 1, 0, 0:PIECE].bitcast(F32), ALU.subtract).then_inc(piece8, 1)
        dve.wait_ge(scr_tab, 16)
        dve.wait_ge(scr_mask, 16)
        dve.memset(y[:, :], 0.0).then_inc(y_zero, 1)

        def lo(out, src, high, done):
            dve.tensor_tensor(out, src, high.bitcast(F32), ALU.subtract).then_inc(done, 1)

        def gcol_piece(n, part):
            if isinstance(n, int):
                c = ((n // NB) % 2 * 2 + part) * WCOLS + (n % NB) * PIECE
                return w_cols[:, c:c + PIECE]
            return w_cols[:, bass.ds((n // NB) % 2 * (2 * WCOLS) + (n % NB) * PIECE + part * WCOLS, PIECE)]

        def step(s, p, split):
            a, sc, pv, wo = stages(s)
            q = 1 - p
            fills = fills_before(s)
            if a:
                dve.wait_ge(act_sq, s + 2)
                need(dve, pool_ms, s + 1)
                dve.tensor_reduce(ms[:, 0:REP + 1], sq[:, :, :], AX.X, ALU.add).then_inc(dve_ms, 1)
                dve.wait_ge(pk_land[q], (s + 1 - q) * 16 + 32)
                need(dve, pool_sum, s + 1)
                for heads, first, n in ((0, 0, 1), (1, 2, REP)):
                    src = ps[:, PS_K + heads * P:PS_K + (heads + n) * P].rearrange("p (h d) -> p h d", h=n)
                    half = P // 2

                    def table(i, lo_, hi_):
                        return tab[:, q, i:i + 1, lo_:hi_].to_broadcast([P, n, hi_ - lo_])
                    dve.tensor_tensor(ra[:, heads:heads + n, :], src, table(first, 0, P), ALU.mult)
                    dve.tensor_tensor(rb[:, heads:heads + n, 0:half], src[:, :, half:P], table(first + 1, 0, half), ALU.mult)
                    last = dve.tensor_tensor(rb[:, heads:heads + n, half:P], src[:, :, 0:half], table(first + 1, half, P), ALU.mult)
                last.then_inc(dve_rope, 1)
            if wo:
                dve.wait_ge(pe_wo, s - 1)
                need(dve, dve_y, s - 2)
                if isinstance(s, int):
                    cols = y[:, (s - 2) % NB * D_MODEL:((s - 2) % NB + 1) * D_MODEL]
                else:
                    cols = y[:, bass.ds((s - 2) % NB * D_MODEL, D_MODEL)]
                dve.tensor_tensor(cols, cols, ps[:, PS_Y:PS_Y + D_MODEL], ALU.add).then_inc(dve_y, 1)
            if sc:
                dve.wait_ge(mask_land[p], (s - p) * 8 + 16)
            for k in range(KB):
                if sc and k < REP:
                    dve.wait_ge(pe_s, s * 4 + (k + 1))
                    plain(dve)
                    dve.tensor_tensor_reduce(out=prob[:, p, k, :], in0=ps[:, PS_S:PS_S + KEYS], in1=mask[:, p, :],
                                             scale=1.0, scalar=-3.0e38, op0=ALU.add, op1=ALU.max,
                                             accum_out=top[:, p, k:k + 1]).then_inc(dve_max, 1)
                    dve.wait_ge(dve_max, s * 4 + (k + 1))
                    dve.tensor_scalar(neg[:, p, k:k + 1], top[:, p, k:k + 1], -SCALE, None, ALU.mult).then_inc(dve_neg, 1)
                if pv:
                    dve.wait_ge(act_hi, fills + (k + 1))
                    lo(pt[:, k % 2, 1, :], ps[:, PS_RING[k % 2]:PS_RING[k % 2] + REP * P], pt[:, k % 2, 0, :], dve_lo)
            n = KB if pv else 0
            if a:
                dve.wait_ge(act_hi, fills + (n + 1))
                lo(kt[:, 1, 0:CACHE], ps[:, PS_RING[1]:PS_RING[1] + CACHE], kt[:, 0, 0:CACHE], dve_lo)
            if pv:
                dve.wait_ge(act_ot, s)
                lo(ot[:, 1, :], ps[:, PS_O:PS_O + REP * P], ot[:, 0, :], dve_ot)
            if a:
                dve.wait_ge(act_hi, fills + (n + 2))
                lo(qt[:, 1, :], ps[:, PS_RING[0]:PS_RING[0] + REP * P], qt[:, 0, :], dve_lo)
                dve.wait_ge(act_hi, fills + (n + 3))
                lo(kt[:, 1, CACHE:KEYS], ps[:, PS_RING[1]:PS_RING[1] + P], kt[:, 0, CACHE:KEYS], dve_lo)
                dve.wait_ge(act_vn, s + 2)
                lo(v[:, q, 1, KBC, :], ps[:, PS_V:PS_V + P], v[:, q, 0, KBC, :], dve_vn)
            if sc:
                dve.wait_ge(act_exp, s * 4 + 4)
                dve.reciprocal(inv[:, p, :], total[:, p, :]).then_inc(dve_inv, 1)
                dve.wait_ge(dve_inv, s + 1)
                for h in range(REP):
                    ins = dve.tensor_scalar(prob[:, p, h, :], prob[:, p, h, :], inv[:, p, h:h + 1], None, ALU.mult)
                ins.then_inc(dve_norm, 1)
                dve.wait_ge(act_vc, s + 1)
                lo(v[:, p, 1, 0:KBC, :], v_raw[:, p, :, :], v[:, p, 0, 0:KBC, :], dve_vc)
            if split:
                dve.wait_ge(act_w, s + 2)
                lo(gcol_piece(s + AHEAD, 1), w_raw[:, p, :], gcol_piece(s + AHEAD, 0), dve_w)

        dve.wait_ge(y_zero, 1)
        over_steps(dve, step)


RANK1, LORAS1 = 32, 16
DD = CH * D_MODEL


def middle(nc, ctx, sems, io, ident, xs, y):
    def sb(name, shape, dt=F32):
        return ctx.enter_context(nc.sbuf_tensor(f"mid_{name}", shape, dt))

    def sem(name):
        return sems.new(f"mid_{name}")

    def pair(name):
        return [sem(f"{name}{i}") for i in range(2)]

    ps = ctx.enter_context(nc.psum_tensor("mid_ps", [P, 4096], F32))
    TR, PA, PB, PC = ((0, 2048), (512, 2560), (1024, 3072), (1536, 3584))

    w0 = sb("w0", [P, DD], F32R)
    wc = sb("wc", [P, 2, DD], F32R)
    wk = sb("wk", [P, 2, DD], F32R)
    wa = sb("wa", [P, 2, DD], F32R)
    wb = sb("wb", [P, 2, DD], F32R)
    was = sb("was", [P, 2, CH * RANK1], F32R)
    wbs = sb("wbs", [RANK1, 2, D_MODEL], F32R)
    was_raw = sb("was_raw", [P, CH * RANK1])
    wbs_raw = sb("wbs_raw", [RANK1, D_MODEL])
    sign = sb("sign", [P, 2, DD], F32R)
    wl = sb("wl", [P, 2, 2, DD], F32R)
    m_raw = sb("m_raw", [P, DD], I32)
    l_raw = sb("l_raw", [P, DD])
    rows = sb("rows", [P, 4, D_MODEL])
    gate = sb("gate", [P, NB, LORAS1])
    coeff = sb("coeff", [P, NB])
    ids = sb("ids", [P, NB], I32)
    ids_f = sb("ids_f", [P, NB])
    lane = sb("lane", [P, 1])
    ids_row = sb("ids_row", [P, NB], I32)
    idx = sb("idx", [P, 2], I32)
    cur = sb("cur", [P, 2, D_MODEL + RANK1])
    at = sb("at", [P, 2, 2, D_MODEL], F32R)
    ats = sb("ats", [RANK1, 2, 2, P], F32R)
    x1 = sb("x1", [P, 2, D_MODEL])
    tmp = sb("tmp", [P, 2, D_MODEL])
    ax = sb("ax", [P, 2, RANK1])
    gb = sb("gb", [P, 2, LORAS1])
    cb = sb("cb", [P, 2])

    small_land, x_land, l_land, m_land = sem("small_land"), sem("x_land"), sem("l_land"), sem("m_land")
    stage_land = [sem(f"stage_land{i}") for i in range(5)]
    stage_hi, stage_lo = sem("stage_hi"), sem("stage_lo")
    pool_lane, pool_ids, pool_idx, pool_one = sem("pool_lane"), sem("pool_ids"), sem("pool_idx1"), sem("pool_one")
    ready, pe_t, act_hi, dve_lo, pe_m = pair("m_ready"), pair("m_pe_t"), pair("m_act_hi"), pair("m_dve_lo"), pair("m_pe_m")
    pe_u, act_hs, dve_ls = pair("m_pe_u"), pair("m_act_hs"), pair("m_dve_ls")
    act_sign, act_wl, dve_wl = sem("act_sign"), sem("act_wl"), sem("dve_wl")
    dve_x1, dve_t, dve_out = pair("m_dve_x1"), pair("m_dve_t"), pair("m_dve_out")
    K = 5
    staged = ("w_sc", "w_ffn1", "w_a1", "w_b1")

    def batch_cols(t, b, n):
        return t[:, bass.ds(b * n, n)]

    block = ctx.enter_context(nc.Block())

    @block.sync
    def _(sp):
        def row(dst, name):
            sp.dma_start(dst, io[name].rearrange("(a n) -> a n", a=1).to_broadcast([dst.shape[0], io[name].shape[0]])).then_inc(small_land, 16)
        row(rows[:, 0, :], "scale0")
        row(rows[:, 1, :], "bias0")
        row(rows[:, 2, :], "bias1c")
        row(rows[:, 3, :], "bias1f")
        row(coeff[:, :], "coeff")
        row(ids[:, :], "ids2")
        sp.dma_start(gate[:, :, :], io["gate1"].rearrange("(a b) n -> a b n", a=1).to_broadcast([P, NB, LORAS1])).then_inc(small_land, 16)
        sp.dma_start(was_raw[:, :], io["w_as1"]).then_inc(small_land, 16)
        sp.dma_start(wbs_raw[:, :], io["w_bs1"]).then_inc(small_land, 16)
        sp.dma_start(xs[:, :], io["x"]).then_inc(x_land, 16)
        sp.dma_start(m_raw[:, :], io["w_int"]).then_inc(stage_land[4], 16)
        for i, name in enumerate(staged):
            if i >= 1:
                sp.wait_ge(stage_hi, i)
                sp.wait_ge(stage_lo, i)
            sp.dma_start(l_raw[:, :], io[name]).then_inc(stage_land[i], 16)
        sp.wait_ge(stage_hi, 5)
        sp.dma_start(m_raw[:, :], io["mask"][0]).then_inc(m_land, 16)
        with sp.Fori(1, NB) as t:
            sp.wait_ge(act_sign, t)
            sp.dma_start(m_raw[:, :], io["mask"][bass.ds(t, 1)].rearrange("a p n -> p (a n)")).then_inc(m_land, 16)

    @block.gpsimd
    def _(pool):
        pool.iota(lane[:, :], [[0, 1]], base=0, channel_multiplier=1, allow_small_or_imprecise_dtypes=True).then_inc(pool_lane, 1)
        pool.wait_ge(pool_lane, 1)
        pool.wait_ge(small_land, 16 * 9)
        pool.tensor_copy(ids_f[:, :], ids[:, :]).then_inc(pool_ids, 1)
        pool.wait_ge(pool_ids, 1)
        pool.tensor_scalar(ids_f[:, :], ids_f[:, :], float(P), lane[:, 0:1], ALU.mult, ALU.add).then_inc(pool_ids, 1)
        pool.wait_ge(pool_ids, 2)
        pool.tensor_copy(ids_row[:, :], ids_f[:, :]).then_inc(pool_ids, 1)
        pool.wait_ge(pool_ids, 3)
        pool.wait_ge(stage_hi, 5)
        pool.wait_ge(stage_lo, 4)

        def gather(t):
            plain(pool)
            pool.tensor_copy(idx[:, 0:1], batch_cols(ids_row, t, 1)).then_inc(pool_idx, 1)
            pool.wait_ge(pool_idx, t + 1)
            plain(pool)
            pool.indirect_dma_start(out=l_raw[:, :], out_offset=None, in_=io["w_adapt"],
                                    in_offset=bass.IndirectOffsetOnAxis(ap=idx[:, 0:1], axis=0)).then_inc(l_land, 16)

        pool.tensor_copy(idx[:, 0:1], ids_row[:, 0:1]).then_inc(pool_idx, 1)
        pool.wait_ge(pool_idx, 1)
        pool.indirect_dma_start(out=l_raw[:, :], out_offset=None, in_=io["w_adapt"],
                                in_offset=bass.IndirectOffsetOnAxis(ap=idx[:, 0:1], axis=0)).then_inc(l_land, 16)
        with pool.Fori(1, NB) as t:
            pool.wait_ge(dve_wl, t)
            pool.wait_ge(l_land, t * 16)
            gather(t)

    @block.tensor
    def _(pe):
        pe.wait_ge(stage_hi, 6)
        pe.wait_ge(stage_lo, 5)

        def product(out, p, w_parts, parts, first=True, last=True, n=D_MODEL):
            for i, (a, b) in enumerate(parts):
                for c in range(CH):
                    mm = pe.matmul(out, at[:, p, a, c * P:(c + 1) * P], w_parts[b][:, c * n:(c + 1) * n],
                                   start=(first and i == 0 and c == 0), stop=(last and i == len(parts) - 1 and c == CH - 1))
            return mm

        def halves(t, *index):
            return [t[(slice(None), *index, part, slice(None))] for part in range(2)]

        with pe.Fori(0, NB // 2) as j:
            for k in range(K):
                for p in range(2):
                    tr, pa, pb, pc = TR[0] if p == 0 else TR[1], PA[p], PB[p], PC[p]
                    pe.wait_ge(ready[p], j * K + (k + 1))
                    for c in range(CH):
                        mm = pe.transpose(ps[:, tr + c * P:tr + (c + 1) * P], cur[:, p, c * P:(c + 1) * P], ident[:, :])
                    if k == 3:
                        mm = pe.transpose(ps[0:RANK1, pc + P:pc + 2 * P], cur[:, p, D_MODEL:D_MODEL + RANK1], ident[:, :])
                    mm.then_inc(pe_t[p], 1)
                for p in range(2):
                    tr, pa, pb, pc = TR[p], PA[p], PB[p], PC[p]
                    pe.wait_ge(dve_lo[p], j * K + (k + 1))
                    out = ps[:, pa:pa + D_MODEL]
                    two = ps[:, pb:pb + D_MODEL]
                    if k == 0:
                        mm = product(out, p, [w0[:, :]], ((0, 0), (1, 0)))
                    if k == 1:
                        pe.wait_ge(act_sign, j * 2 + (p + 1))
                        product(two, p, [sign[:, p, :]], ((0, 0), (1, 0)))
                        mm = product(out, p, halves(wc), PARTS)
                    if k == 2:
                        product(two, p, halves(wa), PARTS)
                        product(ps[:, pc:pc + RANK1], p, halves(was), PARTS, n=RANK1).then_inc(pe_u[p], 1)
                        mm = product(out, p, halves(wk), PARTS, last=False)
                    if k == 3:
                        product(out, p, halves(wb), PARTS, first=False, last=False)
                        pe.wait_ge(dve_ls[p], j + 1)
                        for i, (a, b) in enumerate(PARTS):
                            mm = pe.matmul(out, ats[:, p, a, :], wbs[:, b, :], start=False, stop=(i == 2))
                    if k == 4:
                        pe.wait_ge(dve_wl, j * 2 + (p + 1))
                        mm = product(out, p, halves(wl, p), PARTS)
                    mm.then_inc(pe_m[p], 1)

    @block.scalar
    def _(act):
        def hi(out, src, done):
            act.activation(out, src, ACT.Copy).then_inc(done, 1)
        act.wait_ge(stage_land[4], 16)
        act.wait_ge(small_land, 16 * 9)
        act.activation(w0[:, :], m_raw[:, :], ACT.Copy)
        for i, dst in enumerate((wc, wk, wa, wb)):
            act.wait_ge(stage_land[i], 16)
            if i == 3:
                hi(was[:, 0, :], was_raw[:, :], stage_hi)
                hi(wbs[:, 0, :], wbs_raw[:, :], stage_hi)
            hi(dst[:, 0, :], l_raw[:, :], stage_hi)

        def weights(t, p):
            act.wait_ge(m_land, t * 16 + 16)
            act.activation(sign[:, p, :], m_raw[:, :], ACT.Copy, scale=2.0, bias=-1.0).then_inc(act_sign, 1)

        def adapter(t, p):
            act.wait_ge(l_land, t * 16 + 16)
            hi(wl[:, p, 0, :], l_raw[:, :], act_wl)

        with act.Fori(0, NB // 2) as j:
            for k in range(K):
                for p in range(2):
                    act.wait_ge(pe_t[p], j * K + (k + 1))
                    if k == 3:
                        hi(ats[:, p, 0, :], ps[0:RANK1, PC[p] + P:PC[p] + 2 * P], act_hs[p])
                    hi(at[:, p, 0, :], ps[:, TR[p]:TR[p] + D_MODEL], act_hi[p])
                if k in (0, 2):
                    for p in range(2):
                        if k == 0:
                            weights(j * 2 + p, p)
                        else:
                            adapter(j * 2 + p, p)

    @block.vector
    def _(dve):
        def lo(out, src, high, done):
            dve.tensor_tensor(out, src, high.bitcast(F32), ALU.subtract).then_inc(done, 1)
        for i, dst in enumerate((wc, wk, wa, wb)):
            dve.wait_ge(stage_hi, i + 1 if i < 3 else 6)
            lo(dst[:, 1, :], l_raw[:, :], dst[:, 0, :], stage_lo)
            if i == 3:
                lo(was[:, 1, :], was_raw[:, :], was[:, 0, :], stage_lo)
                lo(wbs[:, 1, :], wbs_raw[:, :], wbs[:, 0, :], stage_lo)
        dve.wait_ge(x_land, 16)

        def step_sem(s):
            return s

        with dve.Fori(0, NB // 2) as j:
            def n(c):
                return j * K + c
            for k in range(K):
                for p in range(2):
                    b = j * 2 + p
                    c0 = cur[:, p, 0:D_MODEL]
                    pa, pb, pc = PA[p], PB[p], PC[p]
                    if k >= 1:
                        if k == 3:
                            dve.wait_ge(pe_u[p], j + 1)
                        else:
                            dve.wait_ge(pe_m[p], n(k))
                    out = ps[:, pa:pa + D_MODEL]
                    t = tmp[:, p, :]
                    if k == 0:
                        dve.tensor_copy(c0, batch_cols(y, b, D_MODEL)).then_inc(ready[p], 1)
                        dve.tensor_tensor(x1[:, p, :], batch_cols(xs, b, D_MODEL), rows[:, 1, :], ALU.add).then_inc(dve_x1[p], 1)
                        dve.tensor_copy(gb[:, p, :], gate[:, bass.ds(b, 1), :].rearrange("p a n -> p (a n)"))
                        dve.tensor_copy(cb[:, p:p + 1], batch_cols(coeff, b, 1)).then_inc(dve_x1[p], 1)
                    if k == 1:
                        dve.tensor_tensor(t, out, rows[:, 0, :], ALU.mult).then_inc(dve_t[p], 1)
                        dve.wait_ge(dve_t[p], j * 5 + 1)
                        dve.wait_ge(dve_x1[p], j * 3 + 2)
                        dve.tensor_tensor(c0, t, x1[:, p, :], ALU.add).then_inc(ready[p], 1)
                    if k == 2:
                        dve.wait_ge(ready[p], n(2))
                        dve.tensor_tensor(x1[:, p, :], c0, rows[:, 3, :], ALU.add).then_inc(dve_x1[p], 1)
                        dve.scalar_tensor_tensor(out=t, in0=ps[:, pb:pb + D_MODEL], scalar=cb[:, p:p + 1], in1=rows[:, 2, :],
                                                 op0=ALU.mult, op1=ALU.add).then_inc(dve_t[p], 1)
                        dve.wait_ge(dve_t[p], j * 5 + 2)
                        dve.wait_ge(dve_x1[p], j * 3 + 3)
                        dve.tensor_tensor(c0, out, t, ALU.add).then_inc(ready[p], 1)
                    if k == 3:
                        gexp = gb[:, p, :].unsqueeze(2).to_broadcast([P, LORAS1, RANK1])
                        dve.tensor_tensor(t.rearrange("p (n r) -> p n r", n=LORAS1),
                                          ps[:, pb:pb + D_MODEL].rearrange("p (n r) -> p n r", n=LORAS1), gexp,
                                          ALU.mult).then_inc(dve_t[p], 1)
                        dve.wait_ge(dve_t[p], j * 5 + 3)
                        dve.tensor_reduce(ax[:, p, :], t.rearrange("p (n r) -> p r n", n=LORAS1), AX.X, ALU.add).then_inc(dve_t[p], 1)
                        dve.wait_ge(dve_t[p], j * 5 + 4)
                        dve.tensor_copy(cur[:, p, D_MODEL:D_MODEL + RANK1], ps[:, pc:pc + RANK1])
                        dve.tensor_tensor(c0.rearrange("p (n r) -> p n r", n=LORAS1),
                                          ax[:, p:p + 1, :].to_broadcast([P, LORAS1, RANK1]), gexp, ALU.mult).then_inc(ready[p], 1)
                    if k == 4:
                        dve.tensor_tensor(c0, out, x1[:, p, :], ALU.add).then_inc(ready[p], 1)
                        dve.wait_ge(ready[p], n(5))
                        plain(dve)
                        dve.tensor_copy(batch_cols(xs, b, D_MODEL), c0).then_inc(dve_t[p], 1)
                for p in range(2):
                    dve.wait_ge(act_hi[p], n(k + 1))
                    lo(at[:, p, 1, :], ps[:, TR[p]:TR[p] + D_MODEL], at[:, p, 0, :], dve_lo[p])
                    if k == 3:
                        dve.wait_ge(act_hs[p], j + 1)
                        lo(ats[:, p, 1, :], ps[0:RANK1, PC[p] + P:PC[p] + 2 * P], ats[:, p, 0, :], dve_ls[p])
                    if k == 2:
                        dve.wait_ge(act_wl, j * 2 + (p + 1))
                        lo(wl[:, p, 1, :], l_raw[:, :], wl[:, p, 0, :], dve_wl)
            for p in range(2):
                dve.wait_ge(pe_m[p], n(K))
                dve.wait_ge(dve_t[p], j * 5 + 5)
                plain(dve)
                dve.tensor_copy(batch_cols(y, j * 2 + p, D_MODEL), ps[:, PA[p]:PA[p] + D_MODEL]).then_inc(dve_out[p], 1)


EXPERTS = 8


def experts(nc, ctx, sems, io, ident, xs, y):
    def sb(name, shape, dt=F32):
        return ctx.enter_context(nc.sbuf_tensor(f"moe_{name}", shape, dt))

    def sem(name):
        return sems.new(f"moe_{name}")

    ps = ctx.enter_context(nc.psum_tensor("moe_ps", [P, 4096], F32))
    ct = sb("ct", [P, NB, 2, D_MODEL], F32R)
    we = sb("we", [P, 2, 2, DD], F32R)
    we_cols = we[:, :, :, :].rearrange("p a b c -> p (a b c)")
    e_raw = sb("e_raw", [P, 2, DD])
    wg_raw = sb("wg_raw", [P, CH * EXPERTS])
    wg = sb("wg", [P, 2, CH * EXPERTS], F32R)
    logit = sb("logit", [P, NB, EXPERTS])
    best = sb("best", [P, NB, 8])
    which = sb("which", [P, NB, 8], mybir.dt.uint32)
    which_f = sb("which_f", [P, NB, 2])
    number = sb("number", [P, EXPERTS])
    gap = sb("gap", [P, NB])
    pr = sb("pr", [P, NB, 2])
    part = sb("part", [P, NB, EXPERTS])
    weight = sb("weight", [P, NB, EXPERTS])

    g_land, e_land = sem("g_land"), [sem(f"e_land{i}") for i in range(2)]
    x_t, x_hi, x_lo, x_g, x_l = sem("x_t"), sem("x_hi"), sem("x_lo"), sem("x_g"), sem("x_l")
    e_hi, e_lo, e_mm, e_acc = sem("e_hi"), sem("e_lo"), sem("e_mm"), sem("e_acc")
    wg_ready, number_ready, top_step, gap_ready, exp_ready, weight_ready = (
        sem(n) for n in ("wg_ready", "number_ready", "top_step", "gap_ready", "exp_ready", "weight_ready"))
    block = ctx.enter_context(nc.Block())

    @block.sync
    def _(sp):
        sp.dma_start(wg_raw[:, :], io["w_gate2"]).then_inc(g_land, 16)
        for e in range(2):
            sp.dma_start(e_raw[:, e, :], io["w_exp"][e]).then_inc(e_land[e], 16)
        with sp.Fori(2, EXPERTS - 1, 2) as e:
            for p in range(2):
                sp.wait_ge(e_lo, e + (p - 1))
                sp.dma_start(e_raw[:, p, :], io["w_exp"][bass.ds(e + p, 1)].rearrange("a p n -> p (a n)")).then_inc(e_land[p], 16)

    @block.gpsimd
    def _(pool):
        pool.iota(number[:, :], [[1, EXPERTS]], base=0, channel_multiplier=0, allow_small_or_imprecise_dtypes=True).then_inc(number_ready, 1)

    @block.tensor
    def _(pe):
        def turn(b):
            if b >= 2:
                pe.wait_ge(x_lo, b - 1)
            bank = (b % 2) * 512
            for c in range(CH):
                mm = pe.transpose(ps[:, bank + c * P:bank + (c + 1) * P], y[:, b * D_MODEL + c * P:b * D_MODEL + (c + 1) * P], ident[:, :])
            mm.then_inc(x_t, 1)

        def gates(b):
            pe.wait_ge(x_lo, b + 1)
            pe.wait_ge(wg_ready, 2)
            if b >= 1:
                pe.wait_ge(x_l, b)
            for i, (a, w_) in enumerate(PARTS):
                for c in range(CH):
                    mm = pe.matmul(ps[:, 1024:1024 + EXPERTS], ct[:, b, a, c * P:(c + 1) * P], wg[:, w_, c * EXPERTS:(c + 1) * EXPERTS],
                                   start=(i == 0 and c == 0), stop=(i == 2 and c == CH - 1))
            mm.then_inc(x_g, 1)

        turn(0)
        for b in range(1, NB):
            turn(b)
            gates(b - 1)
        gates(NB - 1)
        pe.wait_ge(x_l, NB)

        def product(e, b, free):
            free(b)
            for i, (a, w_) in enumerate(PARTS):
                for c in range(CH):
                    if isinstance(e, int):
                        col = (e % 2 * 2 + w_) * DD + c * D_MODEL
                        rhs = we_cols[:, col:col + D_MODEL]
                    else:
                        rhs = we_cols[:, bass.ds(e % 2 * (2 * DD) + (w_ * DD + c * D_MODEL), D_MODEL)]
                    mm = pe.matmul(ps[:, b * 512:(b + 1) * 512], ct[:, b, a, c * P:(c + 1) * P], rhs,
                                   start=(i == 0 and c == 0), stop=(i == 2 and c == CH - 1))
            mm.then_inc(e_mm, 1)

        pe.wait_ge(e_lo, 1)
        for b in range(NB):
            product(0, b, lambda b: None)
        with pe.Fori(1, EXPERTS) as e:
            pe.wait_ge(e_lo, e + 1)
            for b in range(NB):
                product(e, b, lambda b: pe.wait_ge(e_acc, e * NB + (b - NB + 1)))

    @block.scalar
    def _(act):
        def hi(out, src, done):
            act.activation(out, src, ACT.Copy).then_inc(done, 1)
        act.wait_ge(g_land, 16)
        hi(wg[:, 0, :], wg_raw[:, :], wg_ready)
        for b in range(NB):
            act.wait_ge(x_t, b + 1)
            hi(ct[:, b, 0, :], ps[:, (b % 2) * 512:(b % 2) * 512 + D_MODEL], x_hi)
            if b in (3, 6):
                e = b // 3 - 1
                act.wait_ge(e_land[e], 16)
                hi(we[:, e, 0, :], e_raw[:, e, :], e_hi)
        act.wait_ge(gap_ready, 1)
        act.activation(pr[:, :, 1], gap[:, :], ACT.Exp).then_inc(exp_ready, 1)
        with act.Fori(2, EXPERTS - 1, 2) as e:
            for p in range(2):
                act.wait_ge(e_land[p], e * 8 + 16)
                act.wait_ge(e_mm, (e + (p - 1)) * NB)
                hi(we[:, p, 0, :], e_raw[:, p, :], e_hi)

    @block.vector
    def _(dve):
        chain = [0]

        def link(ins):
            chain[0] += 1
            ins.then_inc(top_step, 1)
            dve.wait_ge(top_step, chain[0])

        def lo(out, src, high, done):
            dve.tensor_tensor(out, src, high.bitcast(F32), ALU.subtract).then_inc(done, 1)

        def split_low(e):
            dve.wait_ge(e_hi, e + 1)
            lo(we[:, e, 1, :], e_raw[:, e, :], we[:, e, 0, :], e_lo)

        dve.wait_ge(wg_ready, 1)
        lo(wg[:, 1, :], wg_raw[:, :], wg[:, 0, :], wg_ready)
        for b in range(NB):
            dve.wait_ge(x_hi, b + 1)
            lo(ct[:, b, 1, :], ps[:, (b % 2) * 512:(b % 2) * 512 + D_MODEL], ct[:, b, 0, :], x_lo)
            if b >= 1:
                dve.wait_ge(x_g, b)
                dve.tensor_copy(logit[:, b - 1, :], ps[:, 1024:1024 + EXPERTS]).then_inc(x_l, 1)
            if b in (3, 6):
                split_low(b // 3 - 1)
        dve.wait_ge(x_g, NB)
        dve.tensor_copy(logit[:, NB - 1, :], ps[:, 1024:1024 + EXPERTS]).then_inc(x_l, 1)
        dve.wait_ge(x_l, NB)
        for b in range(NB):
            link(dve.max(best[:, b, :], logit[:, b, :]))
            link(dve.max_index(which[:, b, :], best[:, b, :], logit[:, b, :]))
        dve.tensor_tensor(gap[:, :], best[:, :, 1], best[:, :, 0], ALU.subtract).then_inc(gap_ready, 1)
        link(dve.tensor_copy(which_f[:, :, :], which[:, :, 0:2]))
        dve.wait_ge(number_ready, 1)
        dve.wait_ge(exp_ready, 1)
        link(dve.tensor_scalar(gap[:, :], pr[:, :, 1], 1.0, None, ALU.add))
        link(dve.reciprocal(pr[:, :, 0], gap[:, :]))
        link(dve.tensor_tensor(pr[:, :, 1], pr[:, :, 1], pr[:, :, 0], ALU.mult))
        every = number[:, :].rearrange("p (a e) -> p a e", a=1).to_broadcast([P, NB, EXPERTS])
        for i, dst in ((0, weight), (1, part)):
            link(dve.tensor_tensor(dst[:, :, :], every, which_f[:, :, i:i + 1].to_broadcast([P, NB, EXPERTS]), ALU.is_equal))
            link(dve.tensor_tensor(dst[:, :, :], dst[:, :, :], pr[:, :, i:i + 1].to_broadcast([P, NB, EXPERTS]), ALU.mult))
        dve.tensor_tensor(weight[:, :, :], weight[:, :, :], part[:, :, :], ALU.add).then_inc(weight_ready, 1)
        dve.wait_ge(weight_ready, 1)

        def gather(e, b):
            col = weight[:, b, e:e + 1] if isinstance(e, int) else weight[:, b, bass.ds(e, 1)]
            xb = xs[:, b * D_MODEL:(b + 1) * D_MODEL]
            dve.scalar_tensor_tensor(out=xb, in0=ps[:, b * 512:(b + 1) * 512], scalar=col, in1=xb,
                                     op0=ALU.mult, op1=ALU.add).then_inc(e_acc, 1)

        for e in range(2):
            for b in range(NB):
                dve.wait_ge(e_mm, e * NB + b + 1)
                if e:
                    dve.wait_ge(e_acc, b + 1)
                gather(e, b)
                if e and b == 3:
                    dve.wait_ge(e_hi, 3)
                    lo(we[:, 0, 1, :], e_raw[:, 0, :], we[:, 0, 0, :], e_lo)
        with dve.Fori(2, EXPERTS - 3, 2) as e:
            for p in range(2):
                for b in range(NB):
                    dve.wait_ge(e_mm, (e + p) * NB + (b + 1))
                    dve.wait_ge(e_acc, (e + (p - 1)) * NB + (b + 1))
                    gather(e + p, b)
                    if b == 3:
                        dve.wait_ge(e_hi, e + (p + 2))
                        lo(we[:, 1 - p, 1, :], e_raw[:, 1 - p, :], we[:, 1 - p, 0, :], e_lo)
        for e in range(EXPERTS - 2, EXPERTS):
            for b in range(NB):
                dve.wait_ge(e_mm, e * NB + b + 1)
                dve.wait_ge(e_acc, (e - 1) * NB + b + 1)
                gather(e, b)
                if e == EXPERTS - 2 and b == 3:
                    dve.wait_ge(e_hi, e + 2)
                    lo(we[:, 1, 1, :], e_raw[:, 1, :], we[:, 1, 0, :], e_lo)


FF = 1376
FC = FF // P
FL = FF - FC * P
RANK3, LORA_SCALE3 = 16, 0.5
ACTIVE, RANK_E, SCALING_E, PRIOR_EPS, POOL_E = 4, 8, 2.0, 1e-12, 16
ZC = ACTIVE * RANK_E
ZL = ZC + ACTIVE
GU, CW = 2 * CH * P, 2 * CH * P + D_MODEL
G_AG, G_BD, G_AD = 2 * FF, 2 * FF + 2 * D_MODEL, 2 * FF + 3 * D_MODEL
G_ALL = G_AD + FF
HT = NB // 2
HALF = HT * P


def gated(nc, ctx, sems, io, ident, xs, y):
    def sb(name, shape, dt=F32):
        return ctx.enter_context(nc.sbuf_tensor(f"glu_{name}", shape, dt))

    def sem(name):
        return sems.new(f"glu_{name}")

    xt = sb("xt", [P, 2, CH, NB * P], F32R)
    g = sb("g", [P, G_ALL])
    adt = sb("adt", [P, FC, P])
    t2 = sb("t2", [P, 2, 2, NB * P], F32R)
    bd = sb("bd", [P, 2, D_MODEL], F32R)
    l_gu = sb("l_gu", [P, 2, 2 * CH * FL], F32R)
    l_b = sb("l_b", [P, 2, 2 * FL], F32R)
    l_d = sb("l_d", [FL, 2, D_MODEL], F32R)
    l_a = sb("l_a", [FL, 2, P], F32R)
    w_raw = y[:, 0:2 * CW].rearrange("p (a n) -> p a n", a=2)
    sg, a_f = (y[:, 2 * CW + i * HALF:2 * CW + (i + 1) * HALF] for i in range(2))
    wb = sb("wb", [P, 2, DD], F32R)
    rat = sb("rat", [P, 2, CH * ZL], F32R)
    lbs = sb("lbs", [ZC, 2, D_MODEL], F32R)
    own = sb("own", [P, NB])
    prior = sb("prior", [P, ACTIVE])
    bb = sb("bb", [P, D_MODEL])
    w_land = [sem(f"w3_land{i}") for i in range(2)]
    misc_land, base_land = sem("misc3_land"), sem("base3_land")

    with ExitStack() as c1:
        def sb1(name, shape, dt=F32):
            return c1.enter_context(nc.sbuf_tensor(f"glu_{name}", shape, dt))
        pos = sb1("pos", [P, 5])
        ids = sb1("ids3", [P, NB], I32)
        act_ids = sb1("act_ids", [P, ACTIVE], I32)
        ids_f = sb1("ids3_f", [P, NB])
        acts_f = sb1("acts_f", [P, ACTIVE])
        number = sb1("number3", [P, POOL_E])
        eq = sb1("eq", [P, NB])
        eqa = sb1("eqa", [P, ACTIVE])
        row_f = sb1("row_f", [P, 2])
        idx = sb1("idx3", [P, 2], I32)
        rb = sb1("rb", [P, 2, POOL_E])
        pick = sb1("pick", [P, ACTIVE, POOL_E])
        pickb = sb1("pickb", [P, ACTIVE, POOL_E])
        chosen = sb1("chosen", [P, 2, ACTIVE])
        at = sb1("at3", [P, 2, 2, D_MODEL], F32R)
        tm = sb1("tm", [P, 2, HALF])
        l_raw = sb1("l_raw3", [P, 2 * CH * FL])
        ld_raw = sb1("ld_raw", [FL, D_MODEL])
        wb_raw = sb1("wb_raw", [P, DD])
        ra_raw = sb1("ra_raw", [ZL, D_MODEL])
        lb_raw = sb1("lb_raw", [ZC, D_MODEL])
        ps = c1.enter_context(nc.psum_tensor("glu_ps_a", [P, 4096], F32))
        small_land, g_land, r_land, last_land = sem("s3_land"), sem("g3_land"), sem("r3_land"), sem("l3_land")
        pool_n, chain, idx_ready, act_ln = sem("pool3"), sem("chain3"), sem("idx3_ready"), sem("ln3")
        x_t, x_hi, x_lo = sem("x3_t"), sem("x3_hi"), sem("x3_lo")
        a_t, a_hi, a_lo, d_t, d_cp, r_t, r_hi, r_lo = (sem(n) for n in ("a3_t", "a3_hi", "a3_lo", "d3_t", "d3_cp", "r3_t", "r3_hi", "r3_lo"))
        s_hi, s_lo, t_mm, t_mask, t_hi, t_lo = (sem(n) for n in ("s3_hi", "s3_lo", "t3_mm", "t3_mask", "t3_hi", "t3_lo"))
        X0, A0, D0, R0 = 0, 1024, 2048, 3584
        block = c1.enter_context(nc.Block())

        @block.sync
        def _(sp):
            def row(dst, name):
                sp.dma_start(dst, io[name].rearrange("(a n) -> a n", a=1).to_broadcast([P, io[name].shape[0]])).then_inc(small_land, 16)
            row(ids[:, :], "ids3")
            row(act_ids[:, :], "active")
            sp.dma_start(pos[:, :], io["pos3"]).then_inc(small_land, 16)
            row(rb[:, 0, :], "router_b")
            row(rb[:, 1, :], "prior")
            row(bb[:, :], "b_base")
            for i, (dst, name) in enumerate(((l_raw[:, :], "w3_last"), (ld_raw[:, :], "w3_last_down"))):
                sp.dma_start(dst, io[name]).then_inc(last_land, 16)
            sp.dma_start(wb_raw[:, :], io["w_base"]).then_inc(base_land, 16)
            for p in range(2):
                sp.dma_start(w_raw[:, p, :], io["w3"][p]).then_inc(w_land[p], 16)

        @block.gpsimd
        def _(pool):
            pool.iota(number[:, :], [[1, POOL_E]], base=0, channel_multiplier=0, allow_small_or_imprecise_dtypes=True).then_inc(pool_n, 1)
            pool.wait_ge(idx_ready, 2)
            pool.indirect_dma_start(out=g[:, :], out_offset=None, in_=io["lora3"],
                                    in_offset=bass.IndirectOffsetOnAxis(ap=idx[:, 0:1], axis=0)).then_inc(g_land, 16)
            pool.indirect_dma_start(out=ra_raw[:, :], out_offset=None, in_=io["lora_in"],
                                    in_offset=bass.IndirectOffsetOnAxis(ap=idx[0:ZL, 1:2], axis=0)).then_inc(r_land, 16)
            pool.indirect_dma_start(out=lb_raw[:, :], out_offset=None, in_=io["lora_out"],
                                    in_offset=bass.IndirectOffsetOnAxis(ap=idx[0:ZC, 1:2], axis=0)).then_inc(r_land, 16)

        @block.tensor
        def _(pe):
            for b in range(NB):
                if b >= 2:
                    pe.wait_ge(x_lo, b - 1)
                bank = X0 + (b % 2) * 512
                for c in range(CH):
                    mm = pe.transpose(ps[:, bank + c * P:bank + (c + 1) * P], xs[:, b * D_MODEL + c * P:b * D_MODEL + (c + 1) * P], ident[:, :])
                mm.then_inc(x_t, 1)
            pe.wait_ge(g_land, 16)
            for i in range(2):
                for c in range(CH):
                    col = G_AG + i * D_MODEL + c * P
                    mm = pe.transpose(ps[:, A0 + i * 512 + c * P:A0 + i * 512 + (c + 1) * P], g[:, col:col + P], ident[:, :])
                mm.then_inc(a_t, 1)
            for f in range(FC + 1):
                n = P if f < FC else FL
                mm = pe.transpose(ps[0:n, D0 + f * P:D0 + (f + 1) * P], g[:, G_AD + f * P:G_AD + f * P + n], ident[:, :])
                if f % 4 == 3 or f == FC:
                    mm.then_inc(d_t, 1)
            pe.wait_ge(r_land, 32)
            for c in range(CH):
                mm = pe.transpose(ps[:, R0 + c * ZL:R0 + (c + 1) * ZL], ra_raw[:, c * P:(c + 1) * P], ident[0:ZL, 0:ZL])
            mm.then_inc(r_t, 1)
            pe.wait_ge(x_lo, NB)
            pe.wait_ge(a_lo, 2)
            for n in range(4):
                i, h = n // 2, n % 2
                for q, (a, b) in enumerate(PARTS):
                    for c in range(CH):
                        mm = pe.matmul(ps[:, n * 512:(n + 1) * 512], at[:, i, a, c * P:(c + 1) * P],
                                       xt[:, b, c, h * HALF:(h + 1) * HALF], start=(q == 0 and c == 0), stop=(q == 2 and c == CH - 1))
                mm.then_inc(t_mm, 1)

        @block.scalar
        def _(act):
            def hi(out, src, done):
                act.activation(out, src, ACT.Copy).then_inc(done, 1)
            for b in range(NB):
                act.wait_ge(x_t, b + 1)
                hi(xt[:, 0, :, b * P:(b + 1) * P], ps[:, X0 + (b % 2) * 512:X0 + (b % 2) * 512 + D_MODEL].rearrange("p (c n) -> p c n", c=CH), x_hi)
            for i in range(2):
                act.wait_ge(a_t, i + 1)
                hi(at[:, i, 0, :], ps[:, A0 + i * 512:A0 + i * 512 + D_MODEL], a_hi)
            for i in range(2):
                act.wait_ge(d_t, i + 1)
                hi(adt[:, i * 4:(i + 1) * 4, :], ps[:, D0 + i * 512:D0 + (i + 1) * 512].rearrange("p (c n) -> p c n", c=4), d_cp)
            act.wait_ge(d_t, 3)
            last = D0 + 2 * 512
            hi(adt[:, 8:FC, :], ps[:, last:last + (FC - 8) * P].rearrange("p (c n) -> p c n", c=FC - 8), d_cp)
            hi(l_a[:, 0, :], ps[0:FL, last + (FC - 8) * P:last + (FC - 7) * P], d_cp)
            act.wait_ge(r_t, 1)
            hi(rat[:, 0, :], ps[:, R0:R0 + CH * ZL], r_hi)
            hi(lbs[:, 0, :], lb_raw[:, :], r_hi)
            act.wait_ge(last_land, 32)
            hi(l_gu[:, 0, :], l_raw[:, :], s_hi)
            hi(l_d[:, 0, :], ld_raw[:, :], s_hi)
            hi(l_b[:, 0, :], g[:, 2 * FC * P:2 * FF], s_hi)
            hi(bd[:, 0, :], g[:, G_BD:G_BD + D_MODEL], s_hi)
            act.wait_ge(base_land, 16)
            hi(wb[:, 0, :], wb_raw[:, :], s_hi)
            for n in range(4):
                i, h = n // 2, n % 2
                act.wait_ge(t_mask, n + 1)
                hi(t2[:, i, 0, h * HALF:(h + 1) * HALF], tm[:, n % 2, :], t_hi)
            act.wait_ge(chain, 12)
            act.activation(prior[:, :], chosen[:, 1, :], ACT.Ln).then_inc(act_ln, 1)

        @block.vector
        def _(dve):
            count = [0]

            def link(ins):
                count[0] += 1
                ins.then_inc(chain, 1)
                dve.wait_ge(chain, count[0])

            def lo(out, src, high, done):
                dve.tensor_tensor(out, src, high.bitcast(F32), ALU.subtract).then_inc(done, 1)

            dve.wait_ge(small_land, 16 * 6)
            dve.wait_ge(pool_n, 1)
            dve.tensor_copy(ids_f[:, :], ids[:, :]).then_inc(chain, 1)
            dve.tensor_copy(acts_f[:, :], act_ids[:, :]).then_inc(chain, 1)
            count[0] = 2
            dve.wait_ge(chain, 2)
            link(dve.tensor_scalar(own[:, :], number[:, 0:NB], pos[:, 0:1], None, ALU.is_equal))
            link(dve.tensor_tensor(eq[:, :], own[:, :], ids_f[:, :], ALU.mult))
            link(dve.tensor_scalar(eqa[:, :], number[:, 0:ACTIVE], pos[:, 2:3], None, ALU.is_equal))
            link(dve.tensor_tensor(eqa[:, :], eqa[:, :], acts_f[:, :], ALU.mult))
            link(dve.tensor_reduce(row_f[:, 0:1], eq[:, :], AX.X, ALU.add))
            link(dve.tensor_reduce(row_f[:, 1:2], eqa[:, :], AX.X, ALU.add))
            link(dve.tensor_scalar(row_f[:, 0:1], row_f[:, 0:1], float(RANK3), pos[:, 1:2], ALU.mult, ALU.add))
            link(dve.tensor_scalar(row_f[:, 1:2], row_f[:, 1:2], pos[:, 3:4], pos[:, 4:5], ALU.mult, ALU.add))
            dve.tensor_copy(idx[:, 0:1], row_f[:, 0:1]).then_inc(idx_ready, 1)
            dve.tensor_copy(idx[:, 1:2], row_f[:, 1:2]).then_inc(idx_ready, 1)
            for e in range(ACTIVE):
                ins = dve.tensor_scalar(pick[:, e, :], number[:, :], acts_f[:, e:e + 1], None, ALU.is_equal)
            link(ins)
            for b in range(NB):
                dve.wait_ge(x_hi, b + 1)
                lo(xt[:, 1, :, b * P:(b + 1) * P], ps[:, X0 + (b % 2) * 512:X0 + (b % 2) * 512 + D_MODEL].rearrange("p (c n) -> p c n", c=CH),
                   xt[:, 0, :, b * P:(b + 1) * P], x_lo)
            for i in range(2):
                dve.wait_ge(a_hi, i + 1)
                lo(at[:, i, 1, :], ps[:, A0 + i * 512:A0 + i * 512 + D_MODEL], at[:, i, 0, :], a_lo)
            for i in range(2):
                src = rb[:, i:i + 1, :].to_broadcast([P, ACTIVE, POOL_E])
                dst = (pickb, pick)[i]
                dve.tensor_tensor(dst[:, :, :], pick[:, :, :], src, ALU.mult).then_inc(r_lo, 1)
                dve.wait_ge(r_lo, 2 * i + 1)
                dve.tensor_reduce(chosen[:, i, :], dst[:, :, :], AX.X, ALU.add).then_inc(r_lo, 1)
            dve.wait_ge(r_lo, 4)
            link(dve.tensor_scalar(chosen[:, 1, :], chosen[:, 1, :], PRIOR_EPS, None, ALU.add))
            dve.wait_ge(d_cp, 4)
            last = D0 + 2 * 512 + (FC - 8) * P
            lo(l_a[:, 1, :], ps[0:FL, last:last + P], l_a[:, 0, :], s_lo)
            dve.wait_ge(r_hi, 2)
            lo(rat[:, 1, :], ps[:, R0:R0 + CH * ZL], rat[:, 0, :], s_lo)
            lo(lbs[:, 1, :], lb_raw[:, :], lbs[:, 0, :], s_lo)
            dve.tensor_scalar(own[:, :], own[:, :], LORA_SCALE3, None, ALU.mult).then_inc(r_lo, 1)
            dve.wait_ge(r_lo, 5)
            for n in range(4):
                dve.wait_ge(t_mm, n + 1)
                i, h = n // 2, n % 2
                if n >= 2:
                    dve.wait_ge(t_lo, n - 1)
                mask = own[:, h * HT:(h + 1) * HT].unsqueeze(2).to_broadcast([P, HT, P])
                dve.tensor_tensor(tm[:, n % 2, :].rearrange("p (b n) -> p b n", b=HT), ps[:, n * 512:(n + 1) * 512].rearrange("p (b n) -> p b n", b=HT),
                                  mask, ALU.mult).then_inc(t_mask, 1)
                dve.wait_ge(t_hi, n + 1)
                lo(t2[:, i, 1, h * HALF:(h + 1) * HALF], tm[:, n % 2, :], t2[:, i, 0, h * HALF:(h + 1) * HALF], t_lo)
            for i, (out, src, high) in enumerate(((l_gu[:, 1, :], l_raw[:, :], l_gu[:, 0, :]), (l_d[:, 1, :], ld_raw[:, :], l_d[:, 0, :]),
                                                  (l_b[:, 1, :], g[:, 2 * FC * P:2 * FF], l_b[:, 0, :]),
                                                  (bd[:, 1, :], g[:, G_BD:G_BD + D_MODEL], bd[:, 0, :]),
                                                  (wb[:, 1, :], wb_raw[:, :], wb[:, 0, :]))):
                dve.wait_ge(s_hi, i + 1)
                lo(out, src, high, s_lo)
            dve.wait_ge(act_ln, 1)
            link(dve.tensor_tensor(prior[:, :], prior[:, :], chosen[:, 0, :], ALU.add))

    w_gu = sb("w_gu", [P, 2, 2, GU], F32R)
    w_b = sb("w_b", [P, 2, 2, 2 * P], F32R)
    w_d = sb("w_d", [P, 2, 2, D_MODEL], F32R)
    w_a = sb("w_a", [P, 2, 2, P], F32R)
    a_s = sb("a_s", [P, 2, 2, HALF], F32R)
    td = sb("td", [P, 2, HALF], F32R)
    c3 = sb("c3", [P, 2, CH, HALF], F32R)
    zl = sb("zl", [P, HT, ZL])
    zm = sb("zm", [P, HT])
    zz = sb("zz", [P, HT, ZC])
    zt = td[0:ZC, :, :]
    ps = ctx.enter_context(nc.psum_tensor("glu_ps", [P, 4096], F32))
    PG, PU, PT, PD, PZ = 0, 512, 1024, 2048, 1536
    gu_hi, gu_lo, d_hi, d_lo = sem("gu_hi"), sem("gu_lo"), sem("dn_hi"), sem("dn_lo")
    g_mm, u_mm, d_mm, silu_r, a_r, as_hi, as_lo = (sem(n) for n in ("g_mm", "u_mm", "d_mm", "silu_r", "a_r", "as_hi", "as_lo"))
    td_mask, td_hi, td_lo, o_mm, c_hi, c_lo = (sem(n) for n in ("td_mask", "td_hi", "td_lo", "o_mm", "c_hi", "c_lo"))
    z_mm, z_chain, z_exp, z_ready, z_t, zt_hi, zt_lo, b_mm, out_add, xb = (
        sem(n) for n in ("z_mm", "z_chain", "z_exp", "z_ready", "z_t", "zt_hi", "zt_lo", "b_mm", "out_add", "xb"))
    stored = sem("stored")
    block = ctx.enter_context(nc.Block())
    N = FC + 1

    @block.sync
    def _(sp):
        with sp.Fori(1, FC) as m:
            for p in range(2):
                sp.wait_ge(d_lo, (m * 2 + (p - 1)) * 2)
                f = (m % (FC // 2)) * 2 + p
                sp.dma_start(w_raw[:, p, :], io["w3"][bass.ds(f, 1)].rearrange("a p n -> p (a n)")).then_inc(w_land[p], 16)
        for b in range(NB):
            sp.wait_ge(out_add, b + 1)
            sp.dma_start(io["out"][:, b * D_MODEL:(b + 1) * D_MODEL], xs[:, b * D_MODEL:(b + 1) * D_MODEL]).then_inc(stored, 16)
        sp.wait_ge(stored, 16 * NB)

    @block.gpsimd
    def _(pool):
        for b in range(NB):
            cols = xs[:, b * D_MODEL:(b + 1) * D_MODEL]
            pool.tensor_tensor(cols, cols, bb[:, :], ALU.add).then_inc(xb, 1)

    def chunk_of(h, f):
        return h * N + f

    @block.tensor
    def _(pe):
        def gate_up(h, f, p):
            last = p is None
            n = FL if last else P
            if not last:
                pe.wait_ge(gu_lo, (h * FC + f) * 2 + 2)
            for i, (bank, done, free) in enumerate(((PG, g_mm, silu_r), (PU, u_mm, a_r))):
                if not (isinstance(f, int) and f == 0):
                    pe.wait_ge(free, chunk_of(h, f))
                out = ps[0:n, bank:bank + HALF]
                for q, (a, b) in enumerate(PARTS):
                    for c in range(CH):
                        col = (i * CH + c) * n
                        w = (l_gu[:, a, col:col + n] if last else w_gu[:, p, a, col:col + n])
                        pe.matmul(out, w, xt[:, b, c, bass.ds(h * HALF, HALF)], start=(q == 0 and c == 0), stop=False)
                for q, (a, b) in enumerate(PARTS):
                    w = (l_b[:, a, i * n:(i + 1) * n] if last else w_b[:, p, a, i * n:(i + 1) * n])
                    mm = pe.matmul(out, w, t2[:, i, b, bass.ds(h * HALF, HALF)], start=False, stop=(q == 2))
                mm.then_inc(done, 1)

        def down(h, f, p, first=False):
            last = p is None
            n, ap = (FL, 0) if last else (P, p)
            pe.wait_ge(as_lo, chunk_of(h, f) + 1)
            if not last:
                pe.wait_ge(d_lo, (h * FC + f) * 2 + 2)
            for q, (a, b) in enumerate(PARTS):
                w = l_a[:, a, :] if last else w_a[:, p, a, :]
                pe.matmul(ps[:, PT:PT + HALF], w, a_s[0:n, ap, b, :], start=(first and q == 0), stop=(last and q == 2))
            for c in range(CH):
                for q, (a, b) in enumerate(PARTS):
                    w = (l_d if last else w_d[:, p])[:, a, c * P:(c + 1) * P]
                    mm = pe.matmul(ps[:, PD + c * 512:PD + (c + 1) * 512], w, a_s[0:n, ap, b, :], start=(first and q == 0), stop=False)
            mm.then_inc(d_mm, 1)

        with pe.Fori(0, 2) as h:
            gate_up(h, 0, 0)
            gate_up(h, 1, 1)
            down(h, 0, 0, first=True)
            with pe.Fori(0, (FC - 2) // 2) as j:
                for p in range(2):
                    gate_up(h, j * 2 + (2 + p), p)
                    down(h, j * 2 + (1 + p), 1 - p)
            gate_up(h, FC, None)
            down(h, FC - 1, 1)
            down(h, FC, None)
            pe.wait_ge(td_lo, h + 1)
            for c in range(CH):
                for q, (a, b) in enumerate(PARTS):
                    mm = pe.matmul(ps[:, PD + c * 512:PD + (c + 1) * 512], bd[:, a, c * P:(c + 1) * P], td[:, b, :], start=False, stop=(q == 2))
                mm.then_inc(o_mm, 1)
            pe.wait_ge(c_lo, h * CH + CH)
            for t in range(HT):
                for q, (a, b) in enumerate(PARTS):
                    for c in range(CH):
                        mm = pe.matmul(ps[:, PZ + t * ZL:PZ + (t + 1) * ZL], c3[:, a, c, t * P:(t + 1) * P], rat[:, b, c * ZL:(c + 1) * ZL],
                                       start=(q == 0 and c == 0), stop=(q == 2 and c == CH - 1))
            mm.then_inc(z_mm, 1)
            for t in range(HT):
                for q, (a, b) in enumerate(PARTS):
                    for c in range(CH):
                        pe.matmul(ps[:, PD + t * 512:PD + (t + 1) * 512], c3[:, a, c, t * P:(t + 1) * P], wb[:, b, c * D_MODEL:(c + 1) * D_MODEL],
                                  start=(q == 0 and c == 0), stop=False)
            pe.wait_ge(z_ready, h + 1)
            for t in range(HT):
                mm = pe.transpose(ps[0:ZC, PT + t * P:PT + (t + 1) * P], zz[:, t, :], ident[:, :])
            mm.then_inc(z_t, 1)
            pe.wait_ge(zt_lo, h + 1)
            for t in range(HT):
                for q, (a, b) in enumerate(PARTS):
                    mm = pe.matmul(ps[:, PD + t * 512:PD + (t + 1) * 512], zt[:, a, t * P:(t + 1) * P], lbs[:, b, :], start=False, stop=(q == 2))
                mm.then_inc(b_mm, 1)
            pe.wait_ge(out_add, h * HT + HT)

    Z_STEPS = 8

    @block.scalar
    def _(act):
        def hi(out, src, done):
            act.activation(out, src, ACT.Copy).then_inc(done, 1)

        def split_gu(h, f, m, p):
            act.wait_ge(w_land[p], (h * (FC // 2) + m) * 16 + 16)
            hi(w_gu[:, p, 0, :], w_raw[:, p, 0:GU], gu_hi)
            plain(act)
            hi(w_b[:, p, 0, :], g[:, bass.ds(f * (2 * P), 2 * P)], gu_hi)

        def split_d(f, p):
            hi(w_d[:, p, 0, :], w_raw[:, p, GU:CW], d_hi)
            plain(act)
            hi(w_a[:, p, 0, :], adt_cols[:, bass.ds(f * P, P)], d_hi)

        def slot(h, f, p, ahead=None):
            n, ap = (FL, 0) if p is None else (P, p)
            k = chunk_of(h, f)
            if not (isinstance(f, int) and f < 2):
                act.wait_ge(d_mm, k - 1)
            if p is not None:
                split_d(f, p)
            act.wait_ge(g_mm, k + 1)
            act.activation(sg[0:n, :], ps[0:n, PG:PG + HALF], ACT.Silu).then_inc(silu_r, 1)
            if ahead:
                split_gu(h, *ahead)
            act.wait_ge(a_r, k + 1)
            hi(a_s[0:n, ap, 0, :], a_f[0:n, :], as_hi)

        adt_cols = adt[:, :, :].rearrange("p f n -> p (f n)")
        with act.Fori(0, 2) as h:
            split_gu(h, 0, 0, 0)
            slot(h, 0, 0, (1, 0, 1))
            slot(h, 1, 1, (2, 1, 0))
            with act.Fori(1, FC // 2 - 1) as m:
                slot(h, m * 2, 0, (m * 2 + 1, m, 1))
                slot(h, m * 2 + 1, 1, (m * 2 + 2, m + 1, 0))
            slot(h, FC - 2, 0, (FC - 1, FC // 2 - 1, 1))
            slot(h, FC - 1, 1)
            slot(h, FC, None)
            act.wait_ge(td_mask, h + 1)
            hi(td[:, 0, :], a_f[:, :], td_hi)
            for c in range(CH):
                act.wait_ge(o_mm, h * CH + (c + 1))
                hi(c3[:, 0, c, :], ps[:, PD + c * 512:PD + (c + 1) * 512], c_hi)
            act.wait_ge(z_chain, h * Z_STEPS + 4)
            act.activation(zl[:, :, ZC:ZL], zl[:, :, ZC:ZL], ACT.Exp).then_inc(z_exp, 1)
            act.wait_ge(z_t, h + 1)
            hi(zt[:, 0, :], ps[0:ZC, PT:PT + HALF], zt_hi)

    @block.vector
    def _(dve):
        def lo(out, src, high, done):
            dve.tensor_tensor(out, src, high.bitcast(F32), ALU.subtract).then_inc(done, 1)

        def split_gu(h, f, p):
            dve.wait_ge(gu_hi, (h * FC + f) * 2 + 2)
            lo(w_gu[:, p, 1, :], w_raw[:, p, 0:GU], w_gu[:, p, 0, :], gu_lo)
            plain(dve)
            lo(w_b[:, p, 1, :], g[:, bass.ds(f * (2 * P), 2 * P)], w_b[:, p, 0, :], gu_lo)

        def slot(h, f, p, ahead=None):
            n, ap = (FL, 0) if p is None else (P, p)
            k = chunk_of(h, f)
            if p is not None:
                dve.wait_ge(d_hi, (h * FC + f) * 2 + 2)
                lo(w_d[:, p, 1, :], w_raw[:, p, GU:CW], w_d[:, p, 0, :], d_lo)
                plain(dve)
                lo(w_a[:, p, 1, :], adt_cols[:, bass.ds(f * P, P)], w_a[:, p, 0, :], d_lo)
            if ahead:
                split_gu(h, *ahead)
            dve.wait_ge(silu_r, k + 1)
            dve.wait_ge(u_mm, k + 1)
            if not (isinstance(f, int) and f == 0):
                dve.wait_ge(as_lo, k)
            dve.tensor_tensor(a_f[0:n, :], ps[0:n, PU:PU + HALF], sg[0:n, :], ALU.mult).then_inc(a_r, 1)
            dve.wait_ge(as_hi, k + 1)
            lo(a_s[0:n, ap, 1, :], a_f[0:n, :], a_s[0:n, ap, 0, :], as_lo)

        adt_cols = adt[:, :, :].rearrange("p f n -> p (f n)")
        with dve.Fori(0, 2) as h:
            split_gu(h, 0, 0)
            slot(h, 0, 0, (1, 1))
            slot(h, 1, 1, (2, 0))
            with dve.Fori(1, FC // 2 - 1) as m:
                slot(h, m * 2, 0, (m * 2 + 1, 1))
                slot(h, m * 2 + 1, 1, (m * 2 + 2, 0))
            slot(h, FC - 2, 0, (FC - 1, 1))
            slot(h, FC - 1, 1)
            slot(h, FC, None)
            dve.wait_ge(d_mm, h * N + N)
            dve.wait_ge(as_lo, h * N + N)
            plain(dve)
            dve.tensor_tensor(a_f[:, :].rearrange("p (b n) -> p b n", b=HT), ps[:, PT:PT + HALF].rearrange("p (b n) -> p b n", b=HT),
                              own[:, bass.ds(h * HT, HT)].unsqueeze(2).to_broadcast([P, HT, P]), ALU.mult).then_inc(td_mask, 1)
            dve.wait_ge(td_hi, h + 1)
            lo(td[:, 1, :], a_f[:, :], td[:, 0, :], td_lo)
            for c in range(CH):
                dve.wait_ge(c_hi, h * CH + (c + 1))
                lo(c3[:, 1, c, :], ps[:, PD + c * 512:PD + (c + 1) * 512], c3[:, 0, c, :], c_lo)
            logits = zl[:, :, ZC:ZL]
            peak = zm[:, :].unsqueeze(2).to_broadcast([P, HT, ACTIVE])

            def z_step(n, ins):
                ins.then_inc(z_chain, 1)
                dve.wait_ge(z_chain, h * Z_STEPS + n)
            dve.wait_ge(z_mm, h + 1)
            z_step(1, dve.tensor_copy(zl[:, :, :], ps[:, PZ:PZ + HT * ZL].rearrange("p (t n) -> p t n", t=HT)))
            z_step(2, dve.tensor_tensor(logits, logits, prior[:, :].rearrange("p (a e) -> p a e", a=1).to_broadcast([P, HT, ACTIVE]), ALU.add))
            z_step(3, dve.tensor_reduce(zm[:, :], logits, AX.X, ALU.max))
            dve.tensor_tensor(logits, logits, peak, ALU.subtract).then_inc(z_chain, 1)
            dve.wait_ge(z_exp, h + 1)
            z_step(5, dve.tensor_reduce(zm[:, :], logits, AX.X, ALU.add))
            z_step(6, dve.tensor_scalar(zm[:, :], zm[:, :], 1.0 / SCALING_E, None, ALU.mult))
            z_step(7, dve.reciprocal(zm[:, :], zm[:, :]))
            z_step(8, dve.tensor_tensor(logits, logits, peak, ALU.mult))
            dve.tensor_tensor(zz[:, :, :].rearrange("p t (e r) -> p t e r", e=ACTIVE), zl[:, :, 0:ZC].rearrange("p t (e r) -> p t e r", e=ACTIVE),
                              logits.unsqueeze(3).to_broadcast([P, HT, ACTIVE, RANK_E]), ALU.mult).then_inc(z_ready, 1)
            dve.wait_ge(zt_hi, h + 1)
            lo(zt[:, 1, :], ps[0:ZC, PT:PT + HALF], zt[:, 0, :], zt_lo)
            dve.wait_ge(xb, NB)
            for t in range(HT):
                dve.wait_ge(b_mm, h * HT + (t + 1))
                xh = xs[:, bass.ds((h * HT + t) * D_MODEL, D_MODEL)]
                plain(dve)
                dve.tensor_tensor(xh, xh, ps[:, PD + t * 512:PD + (t + 1) * 512], ALU.add).then_inc(out_add, 1)


def program(nc, io):
    with ExitStack() as whole:
        ident = whole.enter_context(nc.sbuf_tensor("ident", [P, P], F32))
        y = whole.enter_context(nc.sbuf_tensor("y", [P, NB * D_MODEL], F32))

        def layer(build, *buffers):
            sems = Semaphores(nc)
            with ExitStack() as ctx:
                build(nc, ctx, sems, io, ident, *buffers)
            sems.release()

        layer(attention, y)
        xs = whole.enter_context(nc.sbuf_tensor("xs", [P, NB * D_MODEL], F32))
        layer(middle, xs, y)
        layer(experts, xs, y)
        layer(gated, xs, y)


def chunks_of_rows(w):
    r, c = w.shape
    return w.reshape(r // P, P, c).transpose(1, 0, 2).reshape(P, -1)


def layouts(i):
    row = lambda name: i["L3_cond_" + name][0]
    x = i["x"]
    wq = i["L0_cond_Wq"].reshape(HK, REP * P, CH, P).transpose(0, 3, 2, 1).reshape(HK, P, WKV0)
    wk, wv = (i[n].reshape(HK, P, CH, P).transpose(0, 3, 2, 1) for n in ("L0_cond_Wk", "L0_cond_Wv"))
    wkv = np.stack([wv, wk], axis=3).reshape(HK, P, 2 * CH * P)
    wo = i["L0_cond_Wo"].reshape(D_MODEL, HK, REP, P).transpose(1, 3, 2, 0).reshape(HK, P, REP * D_MODEL)
    w_all = np.concatenate([wq, wkv, wo], axis=2).reshape(HK, P, NB, PIECE).transpose(0, 2, 1, 3).reshape(STEPS, P, PIECE)
    ranks = POOL_E * RANK3
    bg, bu = (row(n).transpose(0, 2, 1).reshape(ranks, FF) for n in ("B_gate", "B_up"))
    gate, up, down = (i["L3_cond_W_" + n] for n in ("gate", "up", "down"))
    full = range(0, FC * P, P)
    position = np.arange(P)
    first = position < ZC
    return dict(
        xT=x.reshape(NB, P, CH, P).transpose(3, 0, 2, 1).reshape(P, -1),
        w_all=w_all,
        lens=i["itok_B_207_1644"], block_table=i["itok_Bx16_0_63"],
        k_norm=i["L0_cond_k_norm_w"], q_norm=i["L0_cond_q_norm_w"],
        k_cache=i["L0_cond_k_cache"], v_cache=i["L0_cond_v_cache"],
        inv_freq=(1.0 / 10000.0 ** (np.arange(0, P, 2, dtype=np.float32) / P)).astype(np.float32),
        x=x.transpose(1, 0, 2).reshape(P, -1),
        w_int=chunks_of_rows(i["L0_ffn_weight_int8"].T), scale0=i["L0_ffn_scale"], bias0=i["L0_ffn_bias"],
        w_sc=chunks_of_rows(i["L1_cond_W"].T), bias1c=i["L1_cond_b"], coeff=i["condB_coeff"],
        mask=i["mask_Bx4096x4096_ik1"].reshape(NB, CH, P, D_MODEL).transpose(0, 2, 1, 3).reshape(NB, P, -1),
        gate1=i["L1_ffn_gate"], w_ffn1=chunks_of_rows(i["L1_ffn_kernel"]), bias1f=i["L1_ffn_bias"],
        w_a1=chunks_of_rows(i["L1_ffn_lora_A"].reshape(-1, D_MODEL).T),
        w_b1=chunks_of_rows(i["L1_ffn_lora_B"].transpose(0, 2, 1).reshape(-1, D_MODEL)),
        w_as1=chunks_of_rows(i["L1_ffn_lora_A_shared"].T), w_bs1=i["L1_ffn_lora_B_shared"].T,
        ids2=i["itok_B_3_7"], w_adapt=np.concatenate([chunks_of_rows(w.T) for w in i["L2_cond_weight"]]),
        w_gate2=chunks_of_rows(i["L2_ffn_gate_w"]), w_exp=np.stack([chunks_of_rows(w) for w in i["L2_ffn_expert_w"]]),
        w3=np.stack([np.concatenate([chunks_of_rows(gate[f:f + P].T), chunks_of_rows(up[f:f + P].T), down[:, f:f + P].T], axis=1)
                     for f in full]),
        w3_last=np.concatenate([chunks_of_rows(w[FC * P:].T) for w in (gate, up)], axis=1), w3_last_down=down[:, FC * P:].T,
        lora3=np.concatenate([w[:, f:f + P] for f in range(0, FF, P) for w in (bg, bu)]
                             + [row("A_gate").reshape(ranks, -1), row("A_up").reshape(ranks, -1),
                                row("B_down").transpose(0, 2, 1).reshape(ranks, -1), row("A_down").reshape(ranks, -1)], axis=1),
        ids3=i["itok_B_2_6"], active=i["L3_ffn_active"],
        pos3=np.stack([position // RANK3, position % RANK3, np.where(first, position // RANK_E, position % ZC),
                       np.where(first, RANK_E, 1), np.where(first, position % RANK_E, POOL_E * RANK_E)], axis=1).astype(np.float32),
        router_b=i["L3_ffn_router_b"], prior=i["L3_ffn_domain_prior"],
        w_base=chunks_of_rows(i["L3_ffn_W_base"].T), b_base=i["L3_ffn_b_base"],
        lora_in=np.concatenate([i["L3_ffn_lora_A"].reshape(-1, D_MODEL), i["L3_ffn_router_W"]]),
        lora_out=i["L3_ffn_lora_B"].transpose(0, 2, 1).reshape(-1, D_MODEL),
    )


def kernel(**inputs):
    from concourse import bacc
    from concourse.bass_utils import run_bass_kernel_spmd

    data = {name: np.ascontiguousarray(a) for name, a in layouts({k: np.asarray(v) for k, v in inputs.items()}).items()}
    nc = bacc.Bacc("TRN2", target_bir_lowering=False, num_devices=1)
    io = {name: nc.dram_tensor(f"in_{name}", a.shape, mybir.dt.from_np(a.dtype), kind="ExternalInput").ap() for name, a in data.items()}
    io["out"] = nc.dram_tensor("out_x", (P, NB * D_MODEL), F32, kind="ExternalOutput").ap()
    program(nc, io)
    result = run_bass_kernel_spmd(nc, [{f"in_{name}": a for name, a in data.items()}], core_ids=[0])
    return result.results[0]["out_x"].reshape(P, NB, D_MODEL).transpose(1, 0, 2)
```
